# Optimizing a Trainium2 kernel written in Bass

```python
import numpy as np
import jax
import jax.numpy as jnp

def _softmax(x, axis=-1):
    return jax.nn.softmax(x, axis=axis)
def _gelu(x):
    return jax.nn.gelu(x, approximate=True)
def _silu(x):
    return jax.nn.silu(x)
def _sigmoid(x):
    return jax.nn.sigmoid(x)
def _layernorm(x, axis=-1, eps=1e-5):
    m = jnp.mean(x, axis=axis, keepdims=True)
    v = jnp.var(x, axis=axis, keepdims=True)
    return (x - m) / jnp.sqrt(v + eps)
def _scatter_add(tgt, idx, src, axis=0):
    return tgt.at[idx].add(src)
def _segment_sum(src, seg, n):
    return jax.ops.segment_sum(src, seg, n)

kernel_name = 'mk_rec_standalone_d1_rec_7f5704'

def setup_inputs(seed: int = 0):
    np.random.seed(seed)
    _w = jnp.asarray
    def _rec_inputs():
        import jax
        import jax.numpy as jnp
        _rk = jax.random.key(seed)
        r_uid = jax.random.randint(jax.random.fold_in(_rk, 1), (1024,), 72, 99964, jnp.int32)
        r_mid = jax.random.randint(jax.random.fold_in(_rk, 2), (1024,), 297, 998633, jnp.int32)
        r_cat = jax.random.randint(jax.random.fold_in(_rk, 3), (1024,), 0, 998, jnp.int32)
        r_historical_mid = jnp.stack([jax.random.randint(jax.random.fold_in(jax.random.fold_in(_rk, 4), 0), (1024,), 419, 999446, jnp.int32), jax.random.randint(jax.random.fold_in(jax.random.fold_in(_rk, 4), 1), (1024,), 38, 999969, jnp.int32), jax.random.randint(jax.random.fold_in(jax.random.fold_in(_rk, 4), 2), (1024,), 1969, 998088, jnp.int32), jax.random.randint(jax.random.fold_in(jax.random.fold_in(_rk, 4), 3), (1024,), 487, 999797, jnp.int32), jax.random.randint(jax.random.fold_in(jax.random.fold_in(_rk, 4), 4), (1024,), 1312, 999392, jnp.int32), jax.random.randint(jax.random.fold_in(jax.random.fold_in(_rk, 4), 5), (1024,), 982, 999172, jnp.int32), jax.random.randint(jax.random.fold_in(jax.random.fold_in(_rk, 4), 6), (1024,), 636, 999989, jnp.int32), jax.random.randint(jax.random.fold_in(jax.random.fold_in(_rk, 4), 7), (1024,), 1174, 998009, jnp.int32), jax.random.randint(jax.random.fold_in(jax.random.fold_in(_rk, 4), 8), (1024,), 1830, 997796, jnp.int32), jax.random.randint(jax.random.fold_in(jax.random.fold_in(_rk, 4), 9), (1024,), 1364, 999005, jnp.int32), jax.random.randint(jax.random.fold_in(jax.random.fold_in(_rk, 4), 10), (1024,), 385, 999921, jnp.int32), jax.random.randint(jax.random.fold_in(jax.random.fold_in(_rk, 4), 11), (1024,), 1861, 999457, jnp.int32), jax.random.randint(jax.random.fold_in(jax.random.fold_in(_rk, 4), 12), (1024,), 312, 999813, jnp.int32), jax.random.randint(jax.random.fold_in(jax.random.fold_in(_rk, 4), 13), (1024,), 1292, 998622, jnp.int32), jax.random.randint(jax.random.fold_in(jax.random.fold_in(_rk, 4), 14), (1024,), 227, 999366, jnp.int32), jax.random.randint(jax.random.fold_in(jax.random.fold_in(_rk, 4), 15), (1024,), 6, 999824, jnp.int32), jax.random.randint(jax.random.fold_in(jax.random.fold_in(_rk, 4), 16), (1024,), 66, 999799, jnp.int32), jax.random.randint(jax.random.fold_in(jax.random.fold_in(_rk, 4), 17), (1024,), 135, 999630, jnp.int32), jax.random.randint(jax.random.fold_in(jax.random.fold_in(_rk, 4), 18), (1024,), 790, 999784, jnp.int32), jax.random.randint(jax.random.fold_in(jax.random.fold_in(_rk, 4), 19), (1024,), 1951, 999667, jnp.int32), jax.random.randint(jax.random.fold_in(jax.random.fold_in(_rk, 4), 20), (1024,), 200, 999413, jnp.int32), jax.random.randint(jax.random.fold_in(jax.random.fold_in(_rk, 4), 21), (1024,), 527, 999105, jnp.int32), jax.random.randint(jax.random.fold_in(jax.random.fold_in(_rk, 4), 22), (1024,), 3171, 999978, jnp.int32), jax.random.randint(jax.random.fold_in(jax.random.fold_in(_rk, 4), 23), (1024,), 2377, 998385, jnp.int32), jax.random.randint(jax.random.fold_in(jax.random.fold_in(_rk, 4), 24), (1024,), 2840, 999314, jnp.int32), jax.random.randint(jax.random.fold_in(jax.random.fold_in(_rk, 4), 25), (1024,), 53, 999910, jnp.int32), jax.random.randint(jax.random.fold_in(jax.random.fold_in(_rk, 4), 26), (1024,), 2179, 998624, jnp.int32), jax.random.randint(jax.random.fold_in(jax.random.fold_in(_rk, 4), 27), (1024,), 204, 999372, jnp.int32), jax.random.randint(jax.random.fold_in(jax.random.fold_in(_rk, 4), 28), (1024,), 568, 997425, jnp.int32), jax.random.randint(jax.random.fold_in(jax.random.fold_in(_rk, 4), 29), (1024,), 541, 998315, jnp.int32), jax.random.randint(jax.random.fold_in(jax.random.fold_in(_rk, 4), 30), (1024,), 959, 999892, jnp.int32), jax.random.randint(jax.random.fold_in(jax.random.fold_in(_rk, 4), 31), (1024,), 26, 999709, jnp.int32), jax.random.randint(jax.random.fold_in(jax.random.fold_in(_rk, 4), 32), (1024,), 74, 999511, jnp.int32), jax.random.randint(jax.random.fold_in(jax.random.fold_in(_rk, 4), 33), (1024,), 1313, 997180, jnp.int32), jax.random.randint(jax.random.fold_in(jax.random.fold_in(_rk, 4), 34), (1024,), 369, 999836, jnp.int32), jax.random.randint(jax.random.fold_in(jax.random.fold_in(_rk, 4), 35), (1024,), 150, 999746, jnp.int32), jax.random.randint(jax.random.fold_in(jax.random.fold_in(_rk, 4), 36), (1024,), 1877, 999848, jnp.int32), jax.random.randint(jax.random.fold_in(jax.random.fold_in(_rk, 4), 37), (1024,), 2362, 999959, jnp.int32), jax.random.randint(jax.random.fold_in(jax.random.fold_in(_rk, 4), 38), (1024,), 447, 999958, jnp.int32), jax.random.randint(jax.random.fold_in(jax.random.fold_in(_rk, 4), 39), (1024,), 89, 999884, jnp.int32), jax.random.randint(jax.random.fold_in(jax.random.fold_in(_rk, 4), 40), (1024,), 557, 999483, jnp.int32), jax.random.randint(jax.random.fold_in(jax.random.fold_in(_rk, 4), 41), (1024,), 640, 999902, jnp.int32), jax.random.randint(jax.random.fold_in(jax.random.fold_in(_rk, 4), 42), (1024,), 288, 999401, jnp.int32), jax.random.randint(jax.random.fold_in(jax.random.fold_in(_rk, 4), 43), (1024,), 376, 999986, jnp.int32), jax.random.randint(jax.random.fold_in(jax.random.fold_in(_rk, 4), 44), (1024,), 412, 999406, jnp.int32), jax.random.randint(jax.random.fold_in(jax.random.fold_in(_rk, 4), 45), (1024,), 36, 999732, jnp.int32), jax.random.randint(jax.random.fold_in(jax.random.fold_in(_rk, 4), 46), (1024,), 654, 997679, jnp.int32), jax.random.randint(jax.random.fold_in(jax.random.fold_in(_rk, 4), 47), (1024,), 2931, 998678, jnp.int32), jax.random.randint(jax.random.fold_in(jax.random.fold_in(_rk, 4), 48), (1024,), 768, 999593, jnp.int32), jax.random.randint(jax.random.fold_in(jax.random.fold_in(_rk, 4), 49), (1024,), 4103, 999845, jnp.int32), jax.random.randint(jax.random.fold_in(jax.random.fold_in(_rk, 4), 50), (1024,), 732, 998190, jnp.int32), jax.random.randint(jax.random.fold_in(jax.random.fold_in(_rk, 4), 51), (1024,), 66, 999794, jnp.int32), jax.random.randint(jax.random.fold_in(jax.random.fold_in(_rk, 4), 52), (1024,), 399, 999829, jnp.int32), jax.random.randint(jax.random.fold_in(jax.random.fold_in(_rk, 4), 53), (1024,), 51, 999223, jnp.int32), jax.random.randint(jax.random.fold_in(jax.random.fold_in(_rk, 4), 54), (1024,), 55, 999765, jnp.int32), jax.random.randint(jax.random.fold_in(jax.random.fold_in(_rk, 4), 55), (1024,), 789, 999632, jnp.int32), jax.random.randint(jax.random.fold_in(jax.random.fold_in(_rk, 4), 56), (1024,), 2791, 997377, jnp.int32), jax.random.randint(jax.random.fold_in(jax.random.fold_in(_rk, 4), 57), (1024,), 550, 996808, jnp.int32), jax.random.randint(jax.random.fold_in(jax.random.fold_in(_rk, 4), 58), (1024,), 1954, 999180, jnp.int32), jax.random.randint(jax.random.fold_in(jax.random.fold_in(_rk, 4), 59), (1024,), 2591, 999854, jnp.int32), jax.random.randint(jax.random.fold_in(jax.random.fold_in(_rk, 4), 60), (1024,), 428, 999327, jnp.int32), jax.random.randint(jax.random.fold_in(jax.random.fold_in(_rk, 4), 61), (1024,), 1228, 997009, jnp.int32), jax.random.randint(jax.random.fold_in(jax.random.fold_in(_rk, 4), 62), (1024,), 466, 998562, jnp.int32), jax.random.randint(jax.random.fold_in(jax.random.fold_in(_rk, 4), 63), (1024,), 532, 998538, jnp.int32), jax.random.randint(jax.random.fold_in(jax.random.fold_in(_rk, 4), 64), (1024,), 174, 998862, jnp.int32), jax.random.randint(jax.random.fold_in(jax.random.fold_in(_rk, 4), 65), (1024,), 951, 996205, jnp.int32), jax.random.randint(jax.random.fold_in(jax.random.fold_in(_rk, 4), 66), (1024,), 409, 999531, jnp.int32), jax.random.randint(jax.random.fold_in(jax.random.fold_in(_rk, 4), 67), (1024,), 449, 999793, jnp.int32), jax.random.randint(jax.random.fold_in(jax.random.fold_in(_rk, 4), 68), (1024,), 807, 999481, jnp.int32), jax.random.randint(jax.random.fold_in(jax.random.fold_in(_rk, 4), 69), (1024,), 518, 997969, jnp.int32), jax.random.randint(jax.random.fold_in(jax.random.fold_in(_rk, 4), 70), (1024,), 337, 999753, jnp.int32), jax.random.randint(jax.random.fold_in(jax.random.fold_in(_rk, 4), 71), (1024,), 2064, 997575, jnp.int32), jax.random.randint(jax.random.fold_in(jax.random.fold_in(_rk, 4), 72), (1024,), 1306, 999848, jnp.int32), jax.random.randint(jax.random.fold_in(jax.random.fold_in(_rk, 4), 73), (1024,), 448, 999934, jnp.int32), jax.random.randint(jax.random.fold_in(jax.random.fold_in(_rk, 4), 74), (1024,), 223, 999832, jnp.int32), jax.random.randint(jax.random.fold_in(jax.random.fold_in(_rk, 4), 75), (1024,), 12, 999587, jnp.int32), jax.random.randint(jax.random.fold_in(jax.random.fold_in(_rk, 4), 76), (1024,), 220, 999806, jnp.int32), jax.random.randint(jax.random.fold_in(jax.random.fold_in(_rk, 4), 77), (1024,), 70, 999929, jnp.int32), jax.random.randint(jax.random.fold_in(jax.random.fold_in(_rk, 4), 78), (1024,), 343, 999507, jnp.int32), jax.random.randint(jax.random.fold_in(jax.random.fold_in(_rk, 4), 79), (1024,), 1031, 998900, jnp.int32), jax.random.randint(jax.random.fold_in(jax.random.fold_in(_rk, 4), 80), (1024,), 896, 999764, jnp.int32), jax.random.randint(jax.random.fold_in(jax.random.fold_in(_rk, 4), 81), (1024,), 48, 998947, jnp.int32), jax.random.randint(jax.random.fold_in(jax.random.fold_in(_rk, 4), 82), (1024,), 1279, 999460, jnp.int32), jax.random.randint(jax.random.fold_in(jax.random.fold_in(_rk, 4), 83), (1024,), 461, 999357, jnp.int32), jax.random.randint(jax.random.fold_in(jax.random.fold_in(_rk, 4), 84), (1024,), 974, 999355, jnp.int32), jax.random.randint(jax.random.fold_in(jax.random.fold_in(_rk, 4), 85), (1024,), 158, 998890, jnp.int32), jax.random.randint(jax.random.fold_in(jax.random.fold_in(_rk, 4), 86), (1024,), 246, 998002, jnp.int32), jax.random.randint(jax.random.fold_in(jax.random.fold_in(_rk, 4), 87), (1024,), 371, 998864, jnp.int32), jax.random.randint(jax.random.fold_in(jax.random.fold_in(_rk, 4), 88), (1024,), 1310, 999753, jnp.int32), jax.random.randint(jax.random.fold_in(jax.random.fold_in(_rk, 4), 89), (1024,), 119, 999502, jnp.int32), jax.random.randint(jax.random.fold_in(jax.random.fold_in(_rk, 4), 90), (1024,), 231, 996419, jnp.int32), jax.random.randint(jax.random.fold_in(jax.random.fold_in(_rk, 4), 91), (1024,), 1868, 999626, jnp.int32), jax.random.randint(jax.random.fold_in(jax.random.fold_in(_rk, 4), 92), (1024,), 236, 998008, jnp.int32), jax.random.randint(jax.random.fold_in(jax.random.fold_in(_rk, 4), 93), (1024,), 139, 999055, jnp.int32), jax.random.randint(jax.random.fold_in(jax.random.fold_in(_rk, 4), 94), (1024,), 331, 999951, jnp.int32), jax.random.randint(jax.random.fold_in(jax.random.fold_in(_rk, 4), 95), (1024,), 296, 999680, jnp.int32), jax.random.randint(jax.random.fold_in(jax.random.fold_in(_rk, 4), 96), (1024,), 1790, 999823, jnp.int32), jax.random.randint(jax.random.fold_in(jax.random.fold_in(_rk, 4), 97), (1024,), 1649, 999592, jnp.int32), jax.random.randint(jax.random.fold_in(jax.random.fold_in(_rk, 4), 98), (1024,), 377, 999502, jnp.int32), jax.random.randint(jax.random.fold_in(jax.random.fold_in(_rk, 4), 99), (1024,), 1870, 999985, jnp.int32), jax.random.randint(jax.random.fold_in(jax.random.fold_in(_rk, 4), 100), (1024,), 226, 997941, jnp.int32), jax.random.randint(jax.random.fold_in(jax.random.fold_in(_rk, 4), 101), (1024,), 388, 998897, jnp.int32), jax.random.randint(jax.random.fold_in(jax.random.fold_in(_rk, 4), 102), (1024,), 1600, 999911, jnp.int32), jax.random.randint(jax.random.fold_in(jax.random.fold_in(_rk, 4), 103), (1024,), 1094, 999692, jnp.int32), jax.random.randint(jax.random.fold_in(jax.random.fold_in(_rk, 4), 104), (1024,), 503, 999219, jnp.int32), jax.random.randint(jax.random.fold_in(jax.random.fold_in(_rk, 4), 105), (1024,), 547, 999423, jnp.int32), jax.random.randint(jax.random.fold_in(jax.random.fold_in(_rk, 4), 106), (1024,), 983, 995561, jnp.int32), jax.random.randint(jax.random.fold_in(jax.random.fold_in(_rk, 4), 107), (1024,), 1293, 999581, jnp.int32), jax.random.randint(jax.random.fold_in(jax.random.fold_in(_rk, 4), 108), (1024,), 999, 999887, jnp.int32), jax.random.randint(jax.random.fold_in(jax.random.fold_in(_rk, 4), 109), (1024,), 264, 999676, jnp.int32), jax.random.randint(jax.random.fold_in(jax.random.fold_in(_rk, 4), 110), (1024,), 521, 999341, jnp.int32), jax.random.randint(jax.random.fold_in(jax.random.fold_in(_rk, 4), 111), (1024,), 82, 999001, jnp.int32), jax.random.randint(jax.random.fold_in(jax.random.fold_in(_rk, 4), 112), (1024,), 3521, 999481, jnp.int32), jax.random.randint(jax.random.fold_in(jax.random.fold_in(_rk, 4), 113), (1024,), 127, 999182, jnp.int32), jax.random.randint(jax.random.fold_in(jax.random.fold_in(_rk, 4), 114), (1024,), 428, 999363, jnp.int32), jax.random.randint(jax.random.fold_in(jax.random.fold_in(_rk, 4), 115), (1024,), 131, 998428, jnp.int32), jax.random.randint(jax.random.fold_in(jax.random.fold_in(_rk, 4), 116), (1024,), 871, 999428, jnp.int32), jax.random.randint(jax.random.fold_in(jax.random.fold_in(_rk, 4), 117), (1024,), 731, 999756, jnp.int32), jax.random.randint(jax.random.fold_in(jax.random.fold_in(_rk, 4), 118), (1024,), 154, 999183, jnp.int32), jax.random.randint(jax.random.fold_in(jax.random.fold_in(_rk, 4), 119), (1024,), 1040, 999399, jnp.int32), jax.random.randint(jax.random.fold_in(jax.random.fold_in(_rk, 4), 120), (1024,), 1447, 999736, jnp.int32), jax.random.randint(jax.random.fold_in(jax.random.fold_in(_rk, 4), 121), (1024,), 15, 999722, jnp.int32), jax.random.randint(jax.random.fold_in(jax.random.fold_in(_rk, 4), 122), (1024,), 1783, 999843, jnp.int32), jax.random.randint(jax.random.fold_in(jax.random.fold_in(_rk, 4), 123), (1024,), 792, 999713, jnp.int32), jax.random.randint(jax.random.fold_in(jax.random.fold_in(_rk, 4), 124), (1024,), 415, 998043, jnp.int32), jax.random.randint(jax.random.fold_in(jax.random.fold_in(_rk, 4), 125), (1024,), 1910, 997998, jnp.int32), jax.random.randint(jax.random.fold_in(jax.random.fold_in(_rk, 4), 126), (1024,), 1370, 999233, jnp.int32), jax.random.randint(jax.random.fold_in(jax.random.fold_in(_rk, 4), 127), (1024,), 2354, 999182, jnp.int32), jax.random.randint(jax.random.fold_in(jax.random.fold_in(_rk, 4), 128), (1024,), 50, 999854, jnp.int32), jax.random.randint(jax.random.fold_in(jax.random.fold_in(_rk, 4), 129), (1024,), 346, 999558, jnp.int32), jax.random.randint(jax.random.fold_in(jax.random.fold_in(_rk, 4), 130), (1024,), 64, 999919, jnp.int32), jax.random.randint(jax.random.fold_in(jax.random.fold_in(_rk, 4), 131), (1024,), 2147, 998516, jnp.int32), jax.random.randint(jax.random.fold_in(jax.random.fold_in(_rk, 4), 132), (1024,), 818, 999825, jnp.int32), jax.random.randint(jax.random.fold_in(jax.random.fold_in(_rk, 4), 133), (1024,), 1612, 998470, jnp.int32), jax.random.randint(jax.random.fold_in(jax.random.fold_in(_rk, 4), 134), (1024,), 137, 993603, jnp.int32), jax.random.randint(jax.random.fold_in(jax.random.fold_in(_rk, 4), 135), (1024,), 4, 999516, jnp.int32), jax.random.randint(jax.random.fold_in(jax.random.fold_in(_rk, 4), 136), (1024,), 368, 999894, jnp.int32), jax.random.randint(jax.random.fold_in(jax.random.fold_in(_rk, 4), 137), (1024,), 1538, 999827, jnp.int32), jax.random.randint(jax.random.fold_in(jax.random.fold_in(_rk, 4), 138), (1024,), 1004, 999582, jnp.int32), jax.random.randint(jax.random.fold_in(jax.random.fold_in(_rk, 4), 139), (1024,), 844, 999656, jnp.int32), jax.random.randint(jax.random.fold_in(jax.random.fold_in(_rk, 4), 140), (1024,), 427, 997674, jnp.int32), jax.random.randint(jax.random.fold_in(jax.random.fold_in(_rk, 4), 141), (1024,), 1406, 999517, jnp.int32), jax.random.randint(jax.random.fold_in(jax.random.fold_in(_rk, 4), 142), (1024,), 1186, 999454, jnp.int32), jax.random.randint(jax.random.fold_in(jax.random.fold_in(_rk, 4), 143), (1024,), 42, 999209, jnp.int32), jax.random.randint(jax.random.fold_in(jax.random.fold_in(_rk, 4), 144), (1024,), 1087, 999113, jnp.int32), jax.random.randint(jax.random.fold_in(jax.random.fold_in(_rk, 4), 145), (1024,), 289, 997769, jnp.int32), jax.random.randint(jax.random.fold_in(jax.random.fold_in(_rk, 4), 146), (1024,), 31, 998929, jnp.int32), jax.random.randint(jax.random.fold_in(jax.random.fold_in(_rk, 4), 147), (1024,), 2663, 999504, jnp.int32), jax.random.randint(jax.random.fold_in(jax.random.fold_in(_rk, 4), 148), (1024,), 376, 999964, jnp.int32), jax.random.randint(jax.random.fold_in(jax.random.fold_in(_rk, 4), 149), (1024,), 2067, 997937, jnp.int32), jax.random.randint(jax.random.fold_in(jax.random.fold_in(_rk, 4), 150), (1024,), 185, 999028, jnp.int32), jax.random.randint(jax.random.fold_in(jax.random.fold_in(_rk, 4), 151), (1024,), 3541, 996974, jnp.int32), jax.random.randint(jax.random.fold_in(jax.random.fold_in(_rk, 4), 152), (1024,), 269, 998960, jnp.int32), jax.random.randint(jax.random.fold_in(jax.random.fold_in(_rk, 4), 153), (1024,), 230, 998686, jnp.int32), jax.random.randint(jax.random.fold_in(jax.random.fold_in(_rk, 4), 154), (1024,), 192, 999668, jnp.int32), jax.random.randint(jax.random.fold_in(jax.random.fold_in(_rk, 4), 155), (1024,), 1157, 999662, jnp.int32), jax.random.randint(jax.random.fold_in(jax.random.fold_in(_rk, 4), 156), (1024,), 375, 999531, jnp.int32), jax.random.randint(jax.random.fold_in(jax.random.fold_in(_rk, 4), 157), (1024,), 1563, 999361, jnp.int32), jax.random.randint(jax.random.fold_in(jax.random.fold_in(_rk, 4), 158), (1024,), 1018, 997572, jnp.int32), jax.random.randint(jax.random.fold_in(jax.random.fold_in(_rk, 4), 159), (1024,), 3702, 999694, jnp.int32), jax.random.randint(jax.random.fold_in(jax.random.fold_in(_rk, 4), 160), (1024,), 8, 998414, jnp.int32), jax.random.randint(jax.random.fold_in(jax.random.fold_in(_rk, 4), 161), (1024,), 165, 999293, jnp.int32), jax.random.randint(jax.random.fold_in(jax.random.fold_in(_rk, 4), 162), (1024,), 530, 997990, jnp.int32), jax.random.randint(jax.random.fold_in(jax.random.fold_in(_rk, 4), 163), (1024,), 165, 999121, jnp.int32), jax.random.randint(jax.random.fold_in(jax.random.fold_in(_rk, 4), 164), (1024,), 624, 999206, jnp.int32), jax.random.randint(jax.random.fold_in(jax.random.fold_in(_rk, 4), 165), (1024,), 2163, 999785, jnp.int32), jax.random.randint(jax.random.fold_in(jax.random.fold_in(_rk, 4), 166), (1024,), 2, 997513, jnp.int32), jax.random.randint(jax.random.fold_in(jax.random.fold_in(_rk, 4), 167), (1024,), 712, 998665, jnp.int32), jax.random.randint(jax.random.fold_in(jax.random.fold_in(_rk, 4), 168), (1024,), 19, 997888, jnp.int32), jax.random.randint(jax.random.fold_in(jax.random.fold_in(_rk, 4), 169), (1024,), 1555, 997999, jnp.int32), jax.random.randint(jax.random.fold_in(jax.random.fold_in(_rk, 4), 170), (1024,), 2186, 999590, jnp.int32), jax.random.randint(jax.random.fold_in(jax.random.fold_in(_rk, 4), 171), (1024,), 280, 999979, jnp.int32), jax.random.randint(jax.random.fold_in(jax.random.fold_in(_rk, 4), 172), (1024,), 86, 999070, jnp.int32), jax.random.randint(jax.random.fold_in(jax.random.fold_in(_rk, 4), 173), (1024,), 1040, 999327, jnp.int32), jax.random.randint(jax.random.fold_in(jax.random.fold_in(_rk, 4), 174), (1024,), 398, 998549, jnp.int32), jax.random.randint(jax.random.fold_in(jax.random.fold_in(_rk, 4), 175), (1024,), 2543, 998991, jnp.int32), jax.random.randint(jax.random.fold_in(jax.random.fold_in(_rk, 4), 176), (1024,), 1447, 997884, jnp.int32), jax.random.randint(jax.random.fold_in(jax.random.fold_in(_rk, 4), 177), (1024,), 136, 999211, jnp.int32), jax.random.randint(jax.random.fold_in(jax.random.fold_in(_rk, 4), 178), (1024,), 2508, 999990, jnp.int32), jax.random.randint(jax.random.fold_in(jax.random.fold_in(_rk, 4), 179), (1024,), 340, 999708, jnp.int32), jax.random.randint(jax.random.fold_in(jax.random.fold_in(_rk, 4), 180), (1024,), 748, 999659, jnp.int32), jax.random.randint(jax.random.fold_in(jax.random.fold_in(_rk, 4), 181), (1024,), 1397, 999635, jnp.int32), jax.random.randint(jax.random.fold_in(jax.random.fold_in(_rk, 4), 182), (1024,), 672, 999545, jnp.int32), jax.random.randint(jax.random.fold_in(jax.random.fold_in(_rk, 4), 183), (1024,), 338, 999887, jnp.int32), jax.random.randint(jax.random.fold_in(jax.random.fold_in(_rk, 4), 184), (1024,), 40, 999713, jnp.int32), jax.random.randint(jax.random.fold_in(jax.random.fold_in(_rk, 4), 185), (1024,), 1232, 999750, jnp.int32), jax.random.randint(jax.random.fold_in(jax.random.fold_in(_rk, 4), 186), (1024,), 881, 999829, jnp.int32), jax.random.randint(jax.random.fold_in(jax.random.fold_in(_rk, 4), 187), (1024,), 270, 998792, jnp.int32), jax.random.randint(jax.random.fold_in(jax.random.fold_in(_rk, 4), 188), (1024,), 222, 998989, jnp.int32), jax.random.randint(jax.random.fold_in(jax.random.fold_in(_rk, 4), 189), (1024,), 466, 998378, jnp.int32), jax.random.randint(jax.random.fold_in(jax.random.fold_in(_rk, 4), 190), (1024,), 40, 999587, jnp.int32), jax.random.randint(jax.random.fold_in(jax.random.fold_in(_rk, 4), 191), (1024,), 202, 997065, jnp.int32), jax.random.randint(jax.random.fold_in(jax.random.fold_in(_rk, 4), 192), (1024,), 997, 996999, jnp.int32), jax.random.randint(jax.random.fold_in(jax.random.fold_in(_rk, 4), 193), (1024,), 1054, 999839, jnp.int32), jax.random.randint(jax.random.fold_in(jax.random.fold_in(_rk, 4), 194), (1024,), 3885, 998420, jnp.int32), jax.random.randint(jax.random.fold_in(jax.random.fold_in(_rk, 4), 195), (1024,), 537, 997899, jnp.int32), jax.random.randint(jax.random.fold_in(jax.random.fold_in(_rk, 4), 196), (1024,), 3664, 996269, jnp.int32), jax.random.randint(jax.random.fold_in(jax.random.fold_in(_rk, 4), 197), (1024,), 1860, 999344, jnp.int32), jax.random.randint(jax.random.fold_in(jax.random.fold_in(_rk, 4), 198), (1024,), 1428, 998847, jnp.int32), jax.random.randint(jax.random.fold_in(jax.random.fold_in(_rk, 4), 199), (1024,), 989, 999674, jnp.int32)], axis=1)
        r_historical_cat = jnp.stack([jax.random.randint(jax.random.fold_in(jax.random.fold_in(_rk, 5), 0), (1024,), 0, 1000, jnp.int32), jax.random.randint(jax.random.fold_in(jax.random.fold_in(_rk, 5), 1), (1024,), 0, 1000, jnp.int32), jax.random.randint(jax.random.fold_in(jax.random.fold_in(_rk, 5), 2), (1024,), 0, 999, jnp.int32), jax.random.randint(jax.random.fold_in(jax.random.fold_in(_rk, 5), 3), (1024,), 0, 1000, jnp.int32), jax.random.randint(jax.random.fold_in(jax.random.fold_in(_rk, 5), 4), (1024,), 0, 1000, jnp.int32), jax.random.randint(jax.random.fold_in(jax.random.fold_in(_rk, 5), 5), (1024,), 2, 1000, jnp.int32), jax.random.randint(jax.random.fold_in(jax.random.fold_in(_rk, 5), 6), (1024,), 0, 999, jnp.int32), jax.random.randint(jax.random.fold_in(jax.random.fold_in(_rk, 5), 7), (1024,), 0, 999, jnp.int32), jax.random.randint(jax.random.fold_in(jax.random.fold_in(_rk, 5), 8), (1024,), 0, 1000, jnp.int32), jax.random.randint(jax.random.fold_in(jax.random.fold_in(_rk, 5), 9), (1024,), 0, 1000, jnp.int32), jax.random.randint(jax.random.fold_in(jax.random.fold_in(_rk, 5), 10), (1024,), 0, 1000, jnp.int32), jax.random.randint(jax.random.fold_in(jax.random.fold_in(_rk, 5), 11), (1024,), 0, 1000, jnp.int32), jax.random.randint(jax.random.fold_in(jax.random.fold_in(_rk, 5), 12), (1024,), 0, 999, jnp.int32), jax.random.randint(jax.random.fold_in(jax.random.fold_in(_rk, 5), 13), (1024,), 3, 999, jnp.int32), jax.random.randint(jax.random.fold_in(jax.random.fold_in(_rk, 5), 14), (1024,), 0, 1000, jnp.int32), jax.random.randint(jax.random.fold_in(jax.random.fold_in(_rk, 5), 15), (1024,), 0, 1000, jnp.int32), jax.random.randint(jax.random.fold_in(jax.random.fold_in(_rk, 5), 16), (1024,), 1, 1000, jnp.int32), jax.random.randint(jax.random.fold_in(jax.random.fold_in(_rk, 5), 17), (1024,), 1, 998, jnp.int32), jax.random.randint(jax.random.fold_in(jax.random.fold_in(_rk, 5), 18), (1024,), 1, 999, jnp.int32), jax.random.randint(jax.random.fold_in(jax.random.fold_in(_rk, 5), 19), (1024,), 1, 1000, jnp.int32), jax.random.randint(jax.random.fold_in(jax.random.fold_in(_rk, 5), 20), (1024,), 0, 998, jnp.int32), jax.random.randint(jax.random.fold_in(jax.random.fold_in(_rk, 5), 21), (1024,), 0, 1000, jnp.int32), jax.random.randint(jax.random.fold_in(jax.random.fold_in(_rk, 5), 22), (1024,), 0, 1000, jnp.int32), jax.random.randint(jax.random.fold_in(jax.random.fold_in(_rk, 5), 23), (1024,), 0, 1000, jnp.int32), jax.random.randint(jax.random.fold_in(jax.random.fold_in(_rk, 5), 24), (1024,), 0, 1000, jnp.int32), jax.random.randint(jax.random.fold_in(jax.random.fold_in(_rk, 5), 25), (1024,), 1, 1000, jnp.int32), jax.random.randint(jax.random.fold_in(jax.random.fold_in(_rk, 5), 26), (1024,), 0, 1000, jnp.int32), jax.random.randint(jax.random.fold_in(jax.random.fold_in(_rk, 5), 27), (1024,), 0, 1000, jnp.int32), jax.random.randint(jax.random.fold_in(jax.random.fold_in(_rk, 5), 28), (1024,), 0, 999, jnp.int32), jax.random.randint(jax.random.fold_in(jax.random.fold_in(_rk, 5), 29), (1024,), 0, 999, jnp.int32), jax.random.randint(jax.random.fold_in(jax.random.fold_in(_rk, 5), 30), (1024,), 1, 1000, jnp.int32), jax.random.randint(jax.random.fold_in(jax.random.fold_in(_rk, 5), 31), (1024,), 0, 1000, jnp.int32), jax.random.randint(jax.random.fold_in(jax.random.fold_in(_rk, 5), 32), (1024,), 0, 1000, jnp.int32), jax.random.randint(jax.random.fold_in(jax.random.fold_in(_rk, 5), 33), (1024,), 0, 999, jnp.int32), jax.random.randint(jax.random.fold_in(jax.random.fold_in(_rk, 5), 34), (1024,), 0, 1000, jnp.int32), jax.random.randint(jax.random.fold_in(jax.random.fold_in(_rk, 5), 35), (1024,), 0, 1000, jnp.int32), jax.random.randint(jax.random.fold_in(jax.random.fold_in(_rk, 5), 36), (1024,), 1, 1000, jnp.int32), jax.random.randint(jax.random.fold_in(jax.random.fold_in(_rk, 5), 37), (1024,), 0, 1000, jnp.int32), jax.random.randint(jax.random.fold_in(jax.random.fold_in(_rk, 5), 38), (1024,), 0, 1000, jnp.int32), jax.random.randint(jax.random.fold_in(jax.random.fold_in(_rk, 5), 39), (1024,), 1, 1000, jnp.int32), jax.random.randint(jax.random.fold_in(jax.random.fold_in(_rk, 5), 40), (1024,), 0, 998, jnp.int32), jax.random.randint(jax.random.fold_in(jax.random.fold_in(_rk, 5), 41), (1024,), 0, 1000, jnp.int32), jax.random.randint(jax.random.fold_in(jax.random.fold_in(_rk, 5), 42), (1024,), 0, 1000, jnp.int32), jax.random.randint(jax.random.fold_in(jax.random.fold_in(_rk, 5), 43), (1024,), 1, 998, jnp.int32), jax.random.randint(jax.random.fold_in(jax.random.fold_in(_rk, 5), 44), (1024,), 0, 998, jnp.int32), jax.random.randint(jax.random.fold_in(jax.random.fold_in(_rk, 5), 45), (1024,), 1, 1000, jnp.int32), jax.random.randint(jax.random.fold_in(jax.random.fold_in(_rk, 5), 46), (1024,), 0, 1000, jnp.int32), jax.random.randint(jax.random.fold_in(jax.random.fold_in(_rk, 5), 47), (1024,), 0, 1000, jnp.int32), jax.random.randint(jax.random.fold_in(jax.random.fold_in(_rk, 5), 48), (1024,), 0, 1000, jnp.int32), jax.random.randint(jax.random.fold_in(jax.random.fold_in(_rk, 5), 49), (1024,), 1, 1000, jnp.int32), jax.random.randint(jax.random.fold_in(jax.random.fold_in(_rk, 5), 50), (1024,), 0, 999, jnp.int32), jax.random.randint(jax.random.fold_in(jax.random.fold_in(_rk, 5), 51), (1024,), 0, 998, jnp.int32), jax.random.randint(jax.random.fold_in(jax.random.fold_in(_rk, 5), 52), (1024,), 0, 1000, jnp.int32), jax.random.randint(jax.random.fold_in(jax.random.fold_in(_rk, 5), 53), (1024,), 0, 1000, jnp.int32), jax.random.randint(jax.random.fold_in(jax.random.fold_in(_rk, 5), 54), (1024,), 0, 999, jnp.int32), jax.random.randint(jax.random.fold_in(jax.random.fold_in(_rk, 5), 55), (1024,), 1, 996, jnp.int32), jax.random.randint(jax.random.fold_in(jax.random.fold_in(_rk, 5), 56), (1024,), 1, 999, jnp.int32), jax.random.randint(jax.random.fold_in(jax.random.fold_in(_rk, 5), 57), (1024,), 1, 999, jnp.int32), jax.random.randint(jax.random.fold_in(jax.random.fold_in(_rk, 5), 58), (1024,), 0, 1000, jnp.int32), jax.random.randint(jax.random.fold_in(jax.random.fold_in(_rk, 5), 59), (1024,), 0, 999, jnp.int32), jax.random.randint(jax.random.fold_in(jax.random.fold_in(_rk, 5), 60), (1024,), 1, 1000, jnp.int32), jax.random.randint(jax.random.fold_in(jax.random.fold_in(_rk, 5), 61), (1024,), 0, 999, jnp.int32), jax.random.randint(jax.random.fold_in(jax.random.fold_in(_rk, 5), 62), (1024,), 0, 999, jnp.int32), jax.random.randint(jax.random.fold_in(jax.random.fold_in(_rk, 5), 63), (1024,), 0, 1000, jnp.int32), jax.random.randint(jax.random.fold_in(jax.random.fold_in(_rk, 5), 64), (1024,), 0, 1000, jnp.int32), jax.random.randint(jax.random.fold_in(jax.random.fold_in(_rk, 5), 65), (1024,), 0, 1000, jnp.int32), jax.random.randint(jax.random.fold_in(jax.random.fold_in(_rk, 5), 66), (1024,), 0, 1000, jnp.int32), jax.random.randint(jax.random.fold_in(jax.random.fold_in(_rk, 5), 67), (1024,), 1, 998, jnp.int32), jax.random.randint(jax.random.fold_in(jax.random.fold_in(_rk, 5), 68), (1024,), 0, 999, jnp.int32), jax.random.randint(jax.random.fold_in(jax.random.fold_in(_rk, 5), 69), (1024,), 1, 1000, jnp.int32), jax.random.randint(jax.random.fold_in(jax.random.fold_in(_rk, 5), 70), (1024,), 1, 997, jnp.int32), jax.random.randint(jax.random.fold_in(jax.random.fold_in(_rk, 5), 71), (1024,), 0, 1000, jnp.int32), jax.random.randint(jax.random.fold_in(jax.random.fold_in(_rk, 5), 72), (1024,), 0, 999, jnp.int32), jax.random.randint(jax.random.fold_in(jax.random.fold_in(_rk, 5), 73), (1024,), 0, 1000, jnp.int32), jax.random.randint(jax.random.fold_in(jax.random.fold_in(_rk, 5), 74), (1024,), 1, 998, jnp.int32), jax.random.randint(jax.random.fold_in(jax.random.fold_in(_rk, 5), 75), (1024,), 1, 1000, jnp.int32), jax.random.randint(jax.random.fold_in(jax.random.fold_in(_rk, 5), 76), (1024,), 0, 1000, jnp.int32), jax.random.randint(jax.random.fold_in(jax.random.fold_in(_rk, 5), 77), (1024,), 0, 1000, jnp.int32), jax.random.randint(jax.random.fold_in(jax.random.fold_in(_rk, 5), 78), (1024,), 0, 1000, jnp.int32), jax.random.randint(jax.random.fold_in(jax.random.fold_in(_rk, 5), 79), (1024,), 0, 1000, jnp.int32), jax.random.randint(jax.random.fold_in(jax.random.fold_in(_rk, 5), 80), (1024,), 0, 1000, jnp.int32), jax.random.randint(jax.random.fold_in(jax.random.fold_in(_rk, 5), 81), (1024,), 0, 1000, jnp.int32), jax.random.randint(jax.random.fold_in(jax.random.fold_in(_rk, 5), 82), (1024,), 4, 999, jnp.int32), jax.random.randint(jax.random.fold_in(jax.random.fold_in(_rk, 5), 83), (1024,), 1, 1000, jnp.int32), jax.random.randint(jax.random.fold_in(jax.random.fold_in(_rk, 5), 84), (1024,), 0, 1000, jnp.int32), jax.random.randint(jax.random.fold_in(jax.random.fold_in(_rk, 5), 85), (1024,), 0, 996, jnp.int32), jax.random.randint(jax.random.fold_in(jax.random.fold_in(_rk, 5), 86), (1024,), 0, 998, jnp.int32), jax.random.randint(jax.random.fold_in(jax.random.fold_in(_rk, 5), 87), (1024,), 1, 1000, jnp.int32), jax.random.randint(jax.random.fold_in(jax.random.fold_in(_rk, 5), 88), (1024,), 1, 1000, jnp.int32), jax.random.randint(jax.random.fold_in(jax.random.fold_in(_rk, 5), 89), (1024,), 0, 999, jnp.int32), jax.random.randint(jax.random.fold_in(jax.random.fold_in(_rk, 5), 90), (1024,), 1, 1000, jnp.int32), jax.random.randint(jax.random.fold_in(jax.random.fold_in(_rk, 5), 91), (1024,), 1, 999, jnp.int32), jax.random.randint(jax.random.fold_in(jax.random.fold_in(_rk, 5), 92), (1024,), 1, 1000, jnp.int32), jax.random.randint(jax.random.fold_in(jax.random.fold_in(_rk, 5), 93), (1024,), 0, 1000, jnp.int32), jax.random.randint(jax.random.fold_in(jax.random.fold_in(_rk, 5), 94), (1024,), 4, 999, jnp.int32), jax.random.randint(jax.random.fold_in(jax.random.fold_in(_rk, 5), 95), (1024,), 0, 1000, jnp.int32), jax.random.randint(jax.random.fold_in(jax.random.fold_in(_rk, 5), 96), (1024,), 1, 999, jnp.int32), jax.random.randint(jax.random.fold_in(jax.random.fold_in(_rk, 5), 97), (1024,), 0, 999, jnp.int32), jax.random.randint(jax.random.fold_in(jax.random.fold_in(_rk, 5), 98), (1024,), 0, 1000, jnp.int32), jax.random.randint(jax.random.fold_in(jax.random.fold_in(_rk, 5), 99), (1024,), 3, 1000, jnp.int32), jax.random.randint(jax.random.fold_in(jax.random.fold_in(_rk, 5), 100), (1024,), 1, 999, jnp.int32), jax.random.randint(jax.random.fold_in(jax.random.fold_in(_rk, 5), 101), (1024,), 2, 1000, jnp.int32), jax.random.randint(jax.random.fold_in(jax.random.fold_in(_rk, 5), 102), (1024,), 1, 1000, jnp.int32), jax.random.randint(jax.random.fold_in(jax.random.fold_in(_rk, 5), 103), (1024,), 0, 1000, jnp.int32), jax.random.randint(jax.random.fold_in(jax.random.fold_in(_rk, 5), 104), (1024,), 1, 1000, jnp.int32), jax.random.randint(jax.random.fold_in(jax.random.fold_in(_rk, 5), 105), (1024,), 1, 1000, jnp.int32), jax.random.randint(jax.random.fold_in(jax.random.fold_in(_rk, 5), 106), (1024,), 0, 1000, jnp.int32), jax.random.randint(jax.random.fold_in(jax.random.fold_in(_rk, 5), 107), (1024,), 2, 998, jnp.int32), jax.random.randint(jax.random.fold_in(jax.random.fold_in(_rk, 5), 108), (1024,), 1, 999, jnp.int32), jax.random.randint(jax.random.fold_in(jax.random.fold_in(_rk, 5), 109), (1024,), 0, 999, jnp.int32), jax.random.randint(jax.random.fold_in(jax.random.fold_in(_rk, 5), 110), (1024,), 0, 1000, jnp.int32), jax.random.randint(jax.random.fold_in(jax.random.fold_in(_rk, 5), 111), (1024,), 1, 1000, jnp.int32), jax.random.randint(jax.random.fold_in(jax.random.fold_in(_rk, 5), 112), (1024,), 0, 1000, jnp.int32), jax.random.randint(jax.random.fold_in(jax.random.fold_in(_rk, 5), 113), (1024,), 0, 1000, jnp.int32), jax.random.randint(jax.random.fold_in(jax.random.fold_in(_rk, 5), 114), (1024,), 2, 999, jnp.int32), jax.random.randint(jax.random.fold_in(jax.random.fold_in(_rk, 5), 115), (1024,), 0, 999, jnp.int32), jax.random.randint(jax.random.fold_in(jax.random.fold_in(_rk, 5), 116), (1024,), 0, 999, jnp.int32), jax.random.randint(jax.random.fold_in(jax.random.fold_in(_rk, 5), 117), (1024,), 0, 1000, jnp.int32), jax.random.randint(jax.random.fold_in(jax.random.fold_in(_rk, 5), 118), (1024,), 1, 998, jnp.int32), jax.random.randint(jax.random.fold_in(jax.random.fold_in(_rk, 5), 119), (1024,), 0, 1000, jnp.int32), jax.random.randint(jax.random.fold_in(jax.random.fold_in(_rk, 5), 120), (1024,), 0, 1000, jnp.int32), jax.random.randint(jax.random.fold_in(jax.random.fold_in(_rk, 5), 121), (1024,), 0, 1000, jnp.int32), jax.random.randint(jax.random.fold_in(jax.random.fold_in(_rk, 5), 122), (1024,), 0, 1000, jnp.int32), jax.random.randint(jax.random.fold_in(jax.random.fold_in(_rk, 5), 123), (1024,), 1, 997, jnp.int32), jax.random.randint(jax.random.fold_in(jax.random.fold_in(_rk, 5), 124), (1024,), 0, 1000, jnp.int32), jax.random.randint(jax.random.fold_in(jax.random.fold_in(_rk, 5), 125), (1024,), 0, 1000, jnp.int32), jax.random.randint(jax.random.fold_in(jax.random.fold_in(_rk, 5), 126), (1024,), 0, 1000, jnp.int32), jax.random.randint(jax.random.fold_in(jax.random.fold_in(_rk, 5), 127), (1024,), 0, 1000, jnp.int32), jax.random.randint(jax.random.fold_in(jax.random.fold_in(_rk, 5), 128), (1024,), 0, 999, jnp.int32), jax.random.randint(jax.random.fold_in(jax.random.fold_in(_rk, 5), 129), (1024,), 0, 999, jnp.int32), jax.random.randint(jax.random.fold_in(jax.random.fold_in(_rk, 5), 130), (1024,), 0, 999, jnp.int32), jax.random.randint(jax.random.fold_in(jax.random.fold_in(_rk, 5), 131), (1024,), 0, 999, jnp.int32), jax.random.randint(jax.random.fold_in(jax.random.fold_in(_rk, 5), 132), (1024,), 1, 1000, jnp.int32), jax.random.randint(jax.random.fold_in(jax.random.fold_in(_rk, 5), 133), (1024,), 0, 1000, jnp.int32), jax.random.randint(jax.random.fold_in(jax.random.fold_in(_rk, 5), 134), (1024,), 1, 1000, jnp.int32), jax.random.randint(jax.random.fold_in(jax.random.fold_in(_rk, 5), 135), (1024,), 0, 999, jnp.int32), jax.random.randint(jax.random.fold_in(jax.random.fold_in(_rk, 5), 136), (1024,), 0, 999, jnp.int32), jax.random.randint(jax.random.fold_in(jax.random.fold_in(_rk, 5), 137), (1024,), 2, 999, jnp.int32), jax.random.randint(jax.random.fold_in(jax.random.fold_in(_rk, 5), 138), (1024,), 1, 1000, jnp.int32), jax.random.randint(jax.random.fold_in(jax.random.fold_in(_rk, 5), 139), (1024,), 1, 1000, jnp.int32), jax.random.randint(jax.random.fold_in(jax.random.fold_in(_rk, 5), 140), (1024,), 0, 1000, jnp.int32), jax.random.randint(jax.random.fold_in(jax.random.fold_in(_rk, 5), 141), (1024,), 0, 1000, jnp.int32), jax.random.randint(jax.random.fold_in(jax.random.fold_in(_rk, 5), 142), (1024,), 0, 998, jnp.int32), jax.random.randint(jax.random.fold_in(jax.random.fold_in(_rk, 5), 143), (1024,), 0, 1000, jnp.int32), jax.random.randint(jax.random.fold_in(jax.random.fold_in(_rk, 5), 144), (1024,), 3, 997, jnp.int32), jax.random.randint(jax.random.fold_in(jax.random.fold_in(_rk, 5), 145), (1024,), 0, 999, jnp.int32), jax.random.randint(jax.random.fold_in(jax.random.fold_in(_rk, 5), 146), (1024,), 0, 999, jnp.int32), jax.random.randint(jax.random.fold_in(jax.random.fold_in(_rk, 5), 147), (1024,), 0, 999, jnp.int32), jax.random.randint(jax.random.fold_in(jax.random.fold_in(_rk, 5), 148), (1024,), 0, 999, jnp.int32), jax.random.randint(jax.random.fold_in(jax.random.fold_in(_rk, 5), 149), (1024,), 0, 1000, jnp.int32), jax.random.randint(jax.random.fold_in(jax.random.fold_in(_rk, 5), 150), (1024,), 1, 998, jnp.int32), jax.random.randint(jax.random.fold_in(jax.random.fold_in(_rk, 5), 151), (1024,), 0, 1000, jnp.int32), jax.random.randint(jax.random.fold_in(jax.random.fold_in(_rk, 5), 152), (1024,), 0, 1000, jnp.int32), jax.random.randint(jax.random.fold_in(jax.random.fold_in(_rk, 5), 153), (1024,), 0, 996, jnp.int32), jax.random.randint(jax.random.fold_in(jax.random.fold_in(_rk, 5), 154), (1024,), 0, 1000, jnp.int32), jax.random.randint(jax.random.fold_in(jax.random.fold_in(_rk, 5), 155), (1024,), 1, 1000, jnp.int32), jax.random.randint(jax.random.fold_in(jax.random.fold_in(_rk, 5), 156), (1024,), 0, 997, jnp.int32), jax.random.randint(jax.random.fold_in(jax.random.fold_in(_rk, 5), 157), (1024,), 1, 1000, jnp.int32), jax.random.randint(jax.random.fold_in(jax.random.fold_in(_rk, 5), 158), (1024,), 0, 998, jnp.int32), jax.random.randint(jax.random.fold_in(jax.random.fold_in(_rk, 5), 159), (1024,), 0, 999, jnp.int32), jax.random.randint(jax.random.fold_in(jax.random.fold_in(_rk, 5), 160), (1024,), 0, 1000, jnp.int32), jax.random.randint(jax.random.fold_in(jax.random.fold_in(_rk, 5), 161), (1024,), 1, 999, jnp.int32), jax.random.randint(jax.random.fold_in(jax.random.fold_in(_rk, 5), 162), (1024,), 0, 1000, jnp.int32), jax.random.randint(jax.random.fold_in(jax.random.fold_in(_rk, 5), 163), (1024,), 1, 1000, jnp.int32), jax.random.randint(jax.random.fold_in(jax.random.fold_in(_rk, 5), 164), (1024,), 0, 1000, jnp.int32), jax.random.randint(jax.random.fold_in(jax.random.fold_in(_rk, 5), 165), (1024,), 3, 998, jnp.int32), jax.random.randint(jax.random.fold_in(jax.random.fold_in(_rk, 5), 166), (1024,), 0, 1000, jnp.int32), jax.random.randint(jax.random.fold_in(jax.random.fold_in(_rk, 5), 167), (1024,), 2, 1000, jnp.int32), jax.random.randint(jax.random.fold_in(jax.random.fold_in(_rk, 5), 168), (1024,), 0, 999, jnp.int32), jax.random.randint(jax.random.fold_in(jax.random.fold_in(_rk, 5), 169), (1024,), 0, 1000, jnp.int32), jax.random.randint(jax.random.fold_in(jax.random.fold_in(_rk, 5), 170), (1024,), 0, 1000, jnp.int32), jax.random.randint(jax.random.fold_in(jax.random.fold_in(_rk, 5), 171), (1024,), 2, 1000, jnp.int32), jax.random.randint(jax.random.fold_in(jax.random.fold_in(_rk, 5), 172), (1024,), 0, 999, jnp.int32), jax.random.randint(jax.random.fold_in(jax.random.fold_in(_rk, 5), 173), (1024,), 1, 1000, jnp.int32), jax.random.randint(jax.random.fold_in(jax.random.fold_in(_rk, 5), 174), (1024,), 0, 999, jnp.int32), jax.random.randint(jax.random.fold_in(jax.random.fold_in(_rk, 5), 175), (1024,), 0, 1000, jnp.int32), jax.random.randint(jax.random.fold_in(jax.random.fold_in(_rk, 5), 176), (1024,), 2, 1000, jnp.int32), jax.random.randint(jax.random.fold_in(jax.random.fold_in(_rk, 5), 177), (1024,), 0, 1000, jnp.int32), jax.random.randint(jax.random.fold_in(jax.random.fold_in(_rk, 5), 178), (1024,), 0, 1000, jnp.int32), jax.random.randint(jax.random.fold_in(jax.random.fold_in(_rk, 5), 179), (1024,), 0, 999, jnp.int32), jax.random.randint(jax.random.fold_in(jax.random.fold_in(_rk, 5), 180), (1024,), 0, 1000, jnp.int32), jax.random.randint(jax.random.fold_in(jax.random.fold_in(_rk, 5), 181), (1024,), 0, 997, jnp.int32), jax.random.randint(jax.random.fold_in(jax.random.fold_in(_rk, 5), 182), (1024,), 0, 997, jnp.int32), jax.random.randint(jax.random.fold_in(jax.random.fold_in(_rk, 5), 183), (1024,), 0, 1000, jnp.int32), jax.random.randint(jax.random.fold_in(jax.random.fold_in(_rk, 5), 184), (1024,), 0, 1000, jnp.int32), jax.random.randint(jax.random.fold_in(jax.random.fold_in(_rk, 5), 185), (1024,), 1, 1000, jnp.int32), jax.random.randint(jax.random.fold_in(jax.random.fold_in(_rk, 5), 186), (1024,), 2, 999, jnp.int32), jax.random.randint(jax.random.fold_in(jax.random.fold_in(_rk, 5), 187), (1024,), 1, 998, jnp.int32), jax.random.randint(jax.random.fold_in(jax.random.fold_in(_rk, 5), 188), (1024,), 0, 1000, jnp.int32), jax.random.randint(jax.random.fold_in(jax.random.fold_in(_rk, 5), 189), (1024,), 0, 1000, jnp.int32), jax.random.randint(jax.random.fold_in(jax.random.fold_in(_rk, 5), 190), (1024,), 0, 1000, jnp.int32), jax.random.randint(jax.random.fold_in(jax.random.fold_in(_rk, 5), 191), (1024,), 0, 999, jnp.int32), jax.random.randint(jax.random.fold_in(jax.random.fold_in(_rk, 5), 192), (1024,), 0, 1000, jnp.int32), jax.random.randint(jax.random.fold_in(jax.random.fold_in(_rk, 5), 193), (1024,), 1, 1000, jnp.int32), jax.random.randint(jax.random.fold_in(jax.random.fold_in(_rk, 5), 194), (1024,), 1, 1000, jnp.int32), jax.random.randint(jax.random.fold_in(jax.random.fold_in(_rk, 5), 195), (1024,), 0, 997, jnp.int32), jax.random.randint(jax.random.fold_in(jax.random.fold_in(_rk, 5), 196), (1024,), 0, 1000, jnp.int32), jax.random.randint(jax.random.fold_in(jax.random.fold_in(_rk, 5), 197), (1024,), 2, 999, jnp.int32), jax.random.randint(jax.random.fold_in(jax.random.fold_in(_rk, 5), 198), (1024,), 0, 1000, jnp.int32), jax.random.randint(jax.random.fold_in(jax.random.fold_in(_rk, 5), 199), (1024,), 0, 1000, jnp.int32)], axis=1)
        r_mask = jax.random.randint(jax.random.fold_in(_rk, 6), (1024, 200), 0, 2, jnp.int32)
        return r_uid, r_mid, r_cat, r_historical_mid, r_historical_cat, r_mask
    r_uid, r_mid, r_cat, r_historical_mid, r_historical_cat, r_mask = _rec_inputs()
    def _L0_rec_setup():
        import jax, jax.numpy as jnp
        import numpy as np
        B, T, E = (1024, 200, 64)
        NU, NM, NC = (100000, 1000000, 1000)
        D_LAU_IN = 8 * E
        D_MLP_IN = 7 * E
        EPS = 1e-05
        NEG = -2.0 ** 31

        def _bn(x, g, b):
            mu = jnp.mean(x, axis=0)
            var = jnp.var(x, axis=0)
            return (x - mu) * jax.lax.rsqrt(var + EPS) * g + b
        key = jax.random.key(seed)
        ks = jax.random.split(key, 32)
        f = lambda k, shape, s=0.05: jax.random.normal(k, shape, dtype=jnp.float32) * s
        inp = {'uid': jax.random.randint(ks[0], (B,), 0, NU, dtype=jnp.int32), 'mid': jax.random.randint(ks[1], (B,), 0, NM, dtype=jnp.int32), 'cat': jax.random.randint(ks[2], (B,), 0, NC, dtype=jnp.int32), 'historical_mid': jax.random.randint(ks[3], (B, T), 0, NM, dtype=jnp.int32), 'historical_cat': jax.random.randint(ks[4], (B, T), 0, NC, dtype=jnp.int32), 'mask': jax.random.randint(ks[5], (B, T), 0, 2, dtype=jnp.int32), 'user_table': f(ks[6], (NU, E), 0.1), 'mat_table': f(ks[7], (NM, E), 0.1), 'cat_table': f(ks[8], (NC, E), 0.1), 'lau_w1': f(ks[9], (D_LAU_IN, 256)), 'lau_b1': f(ks[10], (256,)), 'lau_w2': f(ks[11], (256, 128)), 'lau_b2': f(ks[12], (128,)), 'lau_w3': f(ks[13], (128, 1)), 'lau_b3': f(ks[14], (1,)), 'bn0_g': jnp.ones((D_MLP_IN,), jnp.float32), 'bn0_b': jnp.zeros((D_MLP_IN,), jnp.float32), 'mlp_w1': f(ks[15], (D_MLP_IN, 512)), 'mlp_b1': f(ks[16], (512,)), 'bn1_g': jnp.ones((512,), jnp.float32), 'bn1_b': jnp.zeros((512,), jnp.float32), 'mlp_w2': f(ks[17], (512, 256)), 'mlp_b2': f(ks[18], (256,)), 'bn2_g': jnp.ones((256,), jnp.float32), 'bn2_b': jnp.zeros((256,), jnp.float32), 'mlp_w3': f(ks[19], (256, 2)), 'mlp_b3': f(ks[20], (2,))}
        return inp
    _L0_rec_all = _L0_rec_setup()
    _L0_rec_in = {k: v for k, v in _L0_rec_all.items() if k in ('user_table', 'mat_table', 'cat_table', 'lau_w1', 'lau_b1', 'lau_w2', 'lau_b2', 'lau_w3', 'lau_b3', 'bn0_g', 'bn0_b', 'mlp_w1', 'mlp_b1', 'bn1_g', 'bn1_b', 'mlp_w2', 'mlp_b2', 'bn2_g', 'bn2_b', 'mlp_w3', 'mlp_b3', )}
    del _L0_rec_all

    return {
        "r_uid": r_uid,
        "r_mid": r_mid,
        "r_cat": r_cat,
        "r_historical_mid": r_historical_mid,
        "r_historical_cat": r_historical_cat,
        "r_mask": r_mask,
        "L0_rec_user_table": _L0_rec_in["user_table"],
        "L0_rec_mat_table": _L0_rec_in["mat_table"],
        "L0_rec_cat_table": _L0_rec_in["cat_table"],
        "L0_rec_lau_w1": _L0_rec_in["lau_w1"],
        "L0_rec_lau_b1": _L0_rec_in["lau_b1"],
        "L0_rec_lau_w2": _L0_rec_in["lau_w2"],
        "L0_rec_lau_b2": _L0_rec_in["lau_b2"],
        "L0_rec_lau_w3": _L0_rec_in["lau_w3"],
        "L0_rec_lau_b3": _L0_rec_in["lau_b3"],
        "L0_rec_bn0_g": _L0_rec_in["bn0_g"],
        "L0_rec_bn0_b": _L0_rec_in["bn0_b"],
        "L0_rec_mlp_w1": _L0_rec_in["mlp_w1"],
        "L0_rec_mlp_b1": _L0_rec_in["mlp_b1"],
        "L0_rec_bn1_g": _L0_rec_in["bn1_g"],
        "L0_rec_bn1_b": _L0_rec_in["bn1_b"],
        "L0_rec_mlp_w2": _L0_rec_in["mlp_w2"],
        "L0_rec_mlp_b2": _L0_rec_in["mlp_b2"],
        "L0_rec_bn2_g": _L0_rec_in["bn2_g"],
        "L0_rec_bn2_b": _L0_rec_in["bn2_b"],
        "L0_rec_mlp_w3": _L0_rec_in["mlp_w3"],
        "L0_rec_mlp_b3": _L0_rec_in["mlp_b3"],
    }

def reference(r_uid, r_mid, r_cat, r_historical_mid, r_historical_cat, r_mask, L0_rec_user_table, L0_rec_mat_table, L0_rec_cat_table, L0_rec_lau_w1, L0_rec_lau_b1, L0_rec_lau_w2, L0_rec_lau_b2, L0_rec_lau_w3, L0_rec_lau_b3, L0_rec_bn0_g, L0_rec_bn0_b, L0_rec_mlp_w1, L0_rec_mlp_b1, L0_rec_bn1_g, L0_rec_bn1_b, L0_rec_mlp_w2, L0_rec_mlp_b2, L0_rec_bn2_g, L0_rec_bn2_b, L0_rec_mlp_w3, L0_rec_mlp_b3):
    import jax
    import jax.numpy as jnp
    def _L0_rec_ref(uid, mid, cat, historical_mid, historical_cat, mask, user_table, mat_table, cat_table, lau_w1, lau_b1, lau_w2, lau_b2, lau_w3, lau_b3, bn0_g, bn0_b, mlp_w1, mlp_b1, bn1_g, bn1_b, mlp_w2, mlp_b2, bn2_g, bn2_b, mlp_w3, mlp_b3):
        import jax, jax.numpy as jnp
        import numpy as np
        B, T, E = (1024, 200, 64)
        NU, NM, NC = (100000, 1000000, 1000)
        D_LAU_IN = 8 * E
        D_MLP_IN = 7 * E
        EPS = 1e-05
        NEG = -2.0 ** 31

        def _bn(x, g, b):
            mu = jnp.mean(x, axis=0)
            var = jnp.var(x, axis=0)
            return (x - mu) * jax.lax.rsqrt(var + EPS) * g + b
        u = user_table[uid]
        cur = jnp.concatenate([mat_table[mid], cat_table[cat]], axis=1)
        hist = jnp.concatenate([mat_table[historical_mid], cat_table[historical_cat]], axis=2)
        maskf = mask.astype(hist.dtype)
        cur_e = jnp.broadcast_to(cur[:, None, :], hist.shape)
        comb = jnp.concatenate([cur_e, hist, cur_e - hist, cur_e * hist], axis=2)
        h = jax.nn.sigmoid(comb @ lau_w1 + lau_b1)
        h = jax.nn.sigmoid(h @ lau_w2 + lau_b2)
        aw = (h @ lau_w3 + lau_b3)[..., 0]
        masked = jnp.where(mask == 1, aw, jnp.asarray(NEG, aw.dtype))
        scores = jax.nn.softmax(masked, axis=-1) * maskf
        lau = jnp.einsum('bt,bte->be', scores, hist)
        hsum = jnp.einsum('bt,bte->be', maskf, hist)
        hmean = hsum / jnp.sum(maskf, axis=1, keepdims=True)
        x = jnp.concatenate([u, cur, lau, hmean], axis=-1)
        x = _bn(x, bn0_g, bn0_b)
        x = jax.nn.leaky_relu(_bn(x @ mlp_w1 + mlp_b1, bn1_g, bn1_b), 0.1)
        x = jax.nn.leaky_relu(_bn(x @ mlp_w2 + mlp_b2, bn2_g, bn2_b), 0.1)
        return x @ mlp_w3 + mlp_b3

    y = _L0_rec_ref(r_uid, r_mid, r_cat, r_historical_mid, r_historical_cat, r_mask, L0_rec_user_table, L0_rec_mat_table, L0_rec_cat_table, L0_rec_lau_w1, L0_rec_lau_b1, L0_rec_lau_w2, L0_rec_lau_b2, L0_rec_lau_w3, L0_rec_lau_b3, L0_rec_bn0_g, L0_rec_bn0_b, L0_rec_mlp_w1, L0_rec_mlp_b1, L0_rec_bn1_g, L0_rec_bn1_b, L0_rec_mlp_w2, L0_rec_mlp_b2, L0_rec_bn2_g, L0_rec_bn2_b, L0_rec_mlp_w3, L0_rec_mlp_b3)
    return y


_drawn_inputs = setup_inputs


def setup_inputs(seed=0):
    import zlib

    import numpy as np

    out = dict(_drawn_inputs(seed))
    spreads = {'L0_rec_bn0_g': (1.0, 0.2),
     'L0_rec_bn0_b': (0.0, 0.8),
     'L0_rec_bn1_g': (1.0, 0.2),
     'L0_rec_bn1_b': (0.0, 0.1),
     'L0_rec_bn2_g': (1.0, 0.2),
     'L0_rec_bn2_b': (0.0, 0.1)}
    factors = {'L0_rec_lau_w1': 8.0,
     'L0_rec_lau_b1': 8.0,
     'L0_rec_lau_w2': 8.0,
     'L0_rec_lau_b2': 8.0,
     'L0_rec_lau_w3': 8.0,
     'L0_rec_mlp_b1': 8.0,
     'L0_rec_mlp_b2': 8.0}
    for name, (base, spread) in spreads.items():
        noise = np.random.default_rng([zlib.crc32(name.encode()), seed]).standard_normal(out[name].shape)
        drawn = base * np.exp(spread * noise) if base else spread * noise
        out[name] = jnp.asarray(drawn.astype(out[name].dtype))
    for name, factor in factors.items():
        out[name] = (out[name] * factor).astype(out[name].dtype)
    return out
```

```python
from contextlib import ExitStack

import concourse.bass as bass
from concourse import mybir

F32 = mybir.dt.float32
I32 = mybir.dt.int32
ALU = mybir.AluOpType
ACT = mybir.ActivationFunctionType
AX = mybir.AxisListType

P = 128
B, T, E = 1024, 200, 64
F = 2 * E
GB = 16
U = P // GB
J = T // U
G = B // GB
RING = 4
PAIRS = GB // 2
NP = 2 * T
H1, H2 = 256, 128
C1 = H1 // P
WR = 4
TPC = 4
CHUNKS = [(j, min(TPC, J - j)) for j in range(0, J, TPC)]
NCH = len(CHUNKS)
BT = B // P
M1, M2, NO = 512, 256, 2
DX = 7 * E
EPS = 1e-5
BIG = 2.0 ** 31
HALF = 512


def build(nc, ins, out):
    with ExitStack() as ctx:
        def sb(name, shape, dt=F32):
            return ctx.enter_context(nc.sbuf_tensor(name, shape, dt))

        def sem(name):
            return ctx.enter_context(nc.semaphore(name))

        w = {k[len("L0_rec_"):]: v for k, v in ins.items() if k.startswith("L0_rec_")}

        idx = sb("idx", [P, RING, 2, J], I32)
        hist = [sb(f"hist{s}", [P, J, F]) for s in range(RING)]
        histT = sb("histT", [P, 2, GB, T])
        h1T = sb("h1T", [P, 2, C1, NP])
        h2T = sb("h2T", [P, 2, GB * T])
        weff = sb("weff", [P, WR, 2, H1])
        wsum = sb("wsum", [P, J, 2, GB])
        xT = sb("xT", [P, 4, B])
        cbT = sb("cbT", [P, C1, B])
        cur_s = sb("cur_s", [P, RING, GB])
        cb_s = sb("cb_s", [P, RING, C1, GB])
        valid = sb("valid", [P, G, J])
        off = sb("off", [P, G, J])
        mraw = off[:, :, :].bitcast(I32)
        maskf = sb("maskf", [P, G, J])
        wmean = sb("wmean", [P, G, J])
        w1 = sb("w1", [P, 4, H1])
        wac = sb("wac", [P, H1])
        wbc = sb("wbc", [P, H1])
        w2 = sb("w2", [P, C1, H2])
        w2h = sb("w2h", [P, C1, H2])
        w3 = sb("w3", [P, 1])
        w3h = sb("w3h", [P, P])
        vec = sb("vec", [P, 8])
        b1v, b2v, b3v = vec[:, 0:2], vec[:, 2:3], vec[:, 3:4]
        b2f, b3f = vec[:, 4:5], vec[:, 5:6]
        onesP = sb("onesP", [P, P])
        neg1 = sb("neg1", [1, 1])
        ident = sb("ident", [P, P])
        same = sb("same", [P, P])
        blk = sb("blk", [P, GB])
        cidx = sb("cidx", [P, 3, BT], I32)
        cnt = sb("cnt", [P, G])
        rcnt = sb("rcnt", [P, G])
        sc = sb("sc", [P, J])
        scm = sb("scm", [P, J])
        ex = sb("ex", [P, J])
        pr = sb("pr", [P, J])
        mx = sb("mx", [P, 1])
        gmx = sb("gmx", [1, P])
        nmx = sb("nmx", [P, 1])
        rs = sb("rs", [P, 1])
        rden = sb("rden", [P, 1])
        w1m = sb("w1m", [P, 4, M1])
        w2m = sb("w2m", [P, M1 // P, M2])
        w3m = sb("w3m", [P, M2 // P, NO])
        gb0 = sb("gb0", [P, 2, 4])
        gb1 = sb("gb1", [P, 3, M1 // P])
        gb2 = sb("gb2", [P, 3, M2 // P])
        b3m = sb("b3m", [P, NO])
        st = sb("st", [P, 4, 2, 6])
        mv = sb("mv", [P, 4, 2])
        bs = sb("bs", [P, 7, 4])
        outs = sb("outs", [P, BT, NO])
        curg = h2T[:, 1, 0:BT * F].rearrange("p (k f) -> p k f", k=BT)
        userg = h2T[:, 1, BT * F:BT * (F + E)].rearrange("p (k f) -> p k f", k=BT)
        y1 = h2T[:, :, :].rearrange("p a n -> p (a n)")[:, 0:4 * B].rearrange("p (c n) -> p c n", c=4)
        y2 = histT[:, :, :, :].rearrange("p a b n -> p (a b n)")[:, 0:2 * B].rearrange("p (c n) -> p c n", c=2)

        ps = [ctx.enter_context(nc.psum_tensor(f"ps{i}", [P, 512], F32)) for i in range(8)]
        def l1_ps(slot, c):
            return ps[2 * slot + c]
        def l2_ps(slot):
            return ps[4 + slot]
        tr_ps = ps[6]
        s_ps = ps[7][:, 0:J]
        sum_ps = ps[7][:, 32:64]
        nmx_ps = ps[7][:, 64:65]
        den_ps = ps[7][:, 65:66]
        mx_ps = ps[7][0:1, P:2 * P]

        gathered = [sem(f"gathered{s}") for s in range(RING)]
        idx_ready = [sem(f"idx_ready{s}") for s in range(RING)]
        hist_free = sem("hist_free")
        gather_begun = sem("gather_begun")
        weights_ready = sem("weights_ready")
        mlp_ready = sem("mlp_ready")
        mask_ready = sem("mask_ready")
        cidx_ready = sem("cidx_ready")
        cur_ready = sem("cur_ready")
        consts0 = sem("consts0")
        consts = sem("consts")
        setup_dve = sem("setup_dve")
        setup_pe = sem("setup_pe")
        tr_done = sem("tr_done")
        tr_out = sem("tr_out")
        cur_out = sem("cur_out")
        weff_ready = sem("weff_ready")
        l1_done = sem("l1_done")
        h1_ready = sem("h1_ready")
        l2_done = sem("l2_done")
        h2_ready = sem("h2_ready")
        l3_done = sem("l3_done")
        biased = sem("biased")
        masked = sem("masked")
        mx_ready = sem("mx_ready")
        mxt_done = sem("mxt_done")
        gmx_ready = sem("gmx_ready")
        nmx_done = sem("nmx_done")
        nmx_ready = sem("nmx_ready")
        exp_done = sem("exp_done")
        den_done = sem("den_done")
        rden_ready = sem("rden_ready")
        pr_ready = sem("pr_ready")
        wsum_ready = sem("wsum_ready")
        sums_out = sem("sums_out")
        bn_dve = sem("bn_dve")
        mlp_pe = sem("mlp_pe")
        mlp_act = sem("mlp_act")
        out_ready = sem("out_ready")
        var_ready = sem("var_ready")
        root_ready = sem("root_ready")
        stored = sem("stored")
        setup_dve_chain = sem("dve_chain")

        mid_v = ins["r_historical_mid"].rearrange("b (u j) -> (b u) j", u=U)
        cat_v = ins["r_historical_cat"].rearrange("b (u j) -> (b u) j", u=U)
        mask_v = ins["r_mask"].rearrange("(g b) (u j) -> (b u) g j", g=G, u=U)

        NWD = 6
        NMD = 15

        block = ctx.enter_context(nc.Block())

        @block.sync
        def _(sp):
            for k, n in enumerate(("r_mid", "r_cat", "r_uid")):
                sp.dma_start(cidx[:, k, :], ins[n].rearrange("(p k) -> p k", k=BT)).then_inc(cidx_ready, 16)
            for s in range(RING):
                sp.dma_start(idx[:, s, 0, :], mid_v[s * P:(s + 1) * P, :]).then_inc(idx_ready[s], 16)
                sp.dma_start(idx[:, s, 1, :], cat_v[s * P:(s + 1) * P, :]).then_inc(idx_ready[s], 16)
            sp.dma_start(w1[:, :, :], w["lau_w1"].rearrange("(c p) n -> p c n", p=P)).then_inc(weights_ready, 16)
            sp.dma_start(w2[:, :, :], w["lau_w2"].rearrange("(c p) n -> p c n", p=P)).then_inc(weights_ready, 16)
            sp.dma_start(w3[:, :], w["lau_w3"]).then_inc(weights_ready, 16)
            sp.dma_start(b1v, w["lau_b1"].rearrange("(c p) -> p c", p=P), allow_slow_non_contiguous=True).then_inc(weights_ready, 16)
            sp.dma_start(b2v, w["lau_b2"].rearrange("(p a) -> p a", a=1)).then_inc(weights_ready, 16)
            sp.dma_start(b3v, w["lau_b3"].rearrange("(a n) -> a n", a=1).broadcast_to([P, 1])).then_inc(weights_ready, 16)
            sp.dma_start(mraw, mask_v).then_inc(mask_ready, 16)
            sp.dma_start(w1m[0:E, 0, :], w["mlp_w1"][0:E, :]).then_inc(mlp_ready, 16)
            sp.dma_start(w1m[:, 1:4, :], w["mlp_w1"][E:DX, :].rearrange("(c p) n -> p c n", p=P)).then_inc(mlp_ready, 16)
            sp.dma_start(w2m[:, :, :], w["mlp_w2"].rearrange("(c p) n -> p c n", p=P)).then_inc(mlp_ready, 16)
            sp.dma_start(w3m[:, :, :], w["mlp_w3"].rearrange("(c p) n -> p c n", p=P)).then_inc(mlp_ready, 16)
            for k, n in enumerate(("bn0_g", "bn0_b")):
                sp.dma_start(gb0[0:E, k, 0:1], w[n][0:E].rearrange("(p a) -> p a", a=1)).then_inc(mlp_ready, 16)
                sp.dma_start(gb0[:, k, 1:4], w[n][E:DX].rearrange("(c p) -> p c", p=P), allow_slow_non_contiguous=True).then_inc(mlp_ready, 16)
            for k, n in enumerate(("bn1_g", "bn1_b", "mlp_b1")):
                sp.dma_start(gb1[:, k, :], w[n].rearrange("(c p) -> p c", p=P), allow_slow_non_contiguous=True).then_inc(mlp_ready, 16)
            for k, n in enumerate(("bn2_g", "bn2_b", "mlp_b2")):
                sp.dma_start(gb2[:, k, :], w[n].rearrange("(c p) -> p c", p=P), allow_slow_non_contiguous=True).then_inc(mlp_ready, 16)
            sp.dma_start(b3m[:, :], w["mlp_b3"].rearrange("(a n) -> a n", a=1).broadcast_to([P, NO])).then_inc(mlp_ready, 16)
            with sp.Fori(1, G // RING) as it:
                for s in range(RING):
                    sp.wait_ge(gathered[s], it * (2 * J * 16))
                    row = it * (RING * P) + s * P
                    sp.dma_start(idx[:, s, 0, :], mid_v[bass.ds(row, P), :]).then_inc(idx_ready[s], 16)
                    sp.dma_start(idx[:, s, 1, :], cat_v[bass.ds(row, P), :]).then_inc(idx_ready[s], 16)
            sp.wait_ge(out_ready, 1)
            sp.dma_start(out.rearrange("(p k) n -> p k n", k=BT), outs[:, :, :]).then_inc(stored, 16)
            sp.wait_ge(stored, 16)

        @block.gpsimd
        def _(pool):
            def gather(dst, table, col, done):
                nc.gpsimd.indirect_dma_start(out=dst, out_offset=None, in_=table,
                                             in_offset=bass.IndirectOffsetOnAxis(ap=col, axis=0)).then_inc(done, 16)

            nc.gpsimd.memset(onesP[:, :], 1.0).then_inc(consts0, 1)
            nc.gpsimd.memset(neg1[:, :], -1.0).then_inc(consts0, 1)
            pool.wait_ge(cidx_ready, 48)
            for k in range(BT):
                gather(curg[:, k, 0:E], w["mat_table"], cidx[:, 0, k:k + 1], cur_ready)
                gather(curg[:, k, E:F], w["cat_table"], cidx[:, 1, k:k + 1], cur_ready)
                gather(userg[:, k, :], w["user_table"], cidx[:, 2, k:k + 1], cur_ready)
            pool.wait_ge(consts0, 2)
            nc.gpsimd.affine_select(out=ident[:, :], in_=onesP[:, :], compare_op=ALU.is_equal, fill=0.0, base=0,
                                    pattern=[[-1, P]], channel_multiplier=1).then_inc(consts0, 1)
            sv = same[:, :].rearrange("p (b u) -> p b u", u=U)
            ov = onesP[:, :].rearrange("p (b u) -> p b u", u=U)
            nc.gpsimd.affine_select(out=sv, in_=ov, compare_op=ALU.is_ge, fill=0.0, base=0,
                                    pattern=[[-U, GB], [0, U]], channel_multiplier=1).then_inc(consts0, 1)
            nc.gpsimd.affine_select(out=blk[:, :], in_=onesP[:, 0:GB], compare_op=ALU.is_ge, fill=0.0, base=0,
                                    pattern=[[-U, GB]], channel_multiplier=1).then_inc(consts0, 1)
            pool.wait_ge(consts0, 5)
            nc.gpsimd.affine_select(out=sv, in_=sv, compare_op=ALU.is_ge, fill=0.0, base=U - 1,
                                    pattern=[[U, GB], [0, U]], channel_multiplier=-1).then_inc(consts, 1)
            nc.gpsimd.affine_select(out=blk[:, :], in_=blk[:, :], compare_op=ALU.is_ge, fill=0.0, base=U - 1,
                                    pattern=[[U, GB]], channel_multiplier=-1).then_inc(consts, 1)

            with pool.Fori(0, G // RING) as it:
                for s in range(RING):
                    pool.wait_ge(idx_ready[s], it * 32 + 32)
                    pool.wait_ge(hist_free, it * RING + (s + 1))
                    pool.sem_inc(gather_begun, 1)
                    for j in range(J):
                        gather(hist[s][:, j, 0:E], w["mat_table"], idx[:, s, 0, j:j + 1], gathered[s])
                        gather(hist[s][:, j, E:F], w["cat_table"], idx[:, s, 1, j:j + 1], gathered[s])

        @block.tensor
        def _(pe):
            mm = nc.tensor.matmul
            pe.sem_inc(hist_free, RING)

            pe.wait_ge(cur_ready, 3 * BT * 16)
            pe.wait_ge(consts0, 5)
            for k in range(BT):
                nc.tensor.transpose(ps[k // 4][:, (k % 4) * P:(k % 4 + 1) * P], curg[:, k, :], ident[:, :])
                t = nc.tensor.transpose(ps[2 + k // 4][0:E, (k % 4) * P:(k % 4 + 1) * P], userg[:, k, :], ident[:, :])
            t.then_inc(setup_pe, 1)
            pe.wait_ge(setup_dve, 1)
            for c in range(C1):
                mm(ps[4][:, 0:1], w2h[:, c, :], onesP[:, 0:1], start=(c == 0), stop=(c == C1 - 1))
            mm(ps[5][:, 0:1], w3h[:, :], onesP[:, 0:1], start=True, stop=True)
            pe.wait_ge(consts, 2)
            mm(ps[5][:, 64:64 + G], same[:, :], cnt[:, :], start=True, stop=True).then_inc(setup_pe, 1)
            pe.wait_ge(setup_dve, 2)
            for c in range(C1):
                for h in range(2):
                    t = mm(ps[2 * c + h][:, :], wac[:, c * P:(c + 1) * P], xT[:, 1, h * HALF:(h + 1) * HALF],
                           start=True, stop=True)
            t.then_inc(setup_pe, 1)
            pe.wait_ge(setup_dve, 3)

            def transpose_chunk(it, s, k):
                n = it * (RING * NCH) + (s * NCH + k)
                if k == 0:
                    pe.wait_ge(gathered[s], it * (2 * J * 16) + 2 * J * 16)
                if not (type(n) is int and n < 1):
                    pe.wait_ge(tr_out, n)
                j0, nj = CHUNKS[k]
                for j in range(nj):
                    t = nc.tensor.transpose(tr_ps[:, j * P:(j + 1) * P], hist[s][:, j0 + j, :], ident[:, :])
                t.then_inc(tr_done, 1)

            def layer2(n, q):
                pe.wait_ge(h1_ready, n + 1)
                if not (type(n) is int and n < 2):
                    pe.wait_ge(h2_ready, n - 1)
                for c in range(C1):
                    t = mm(l2_ps(q % 2)[:, 0:NP], w2h[:, c, :], h1T[:, q % 2, c, :], start=(c == 0), stop=(c == C1 - 1))
                t.then_inc(l2_done, 1)

            def scores(b, bs_):
                pe.wait_ge(h2_ready, b * PAIRS + PAIRS)
                if not (type(b) is int and b < 1):
                    pe.wait_ge(sums_out, b)
                for j in range(J):
                    t = mm(s_ps[:, j:j + 1], h2T[:, bs_ % 2, j * P:(j + 1) * P], w3h[:, 0:1], start=True, stop=True)
                t.then_inc(l3_done, 1)

            def step(it, s, tr, main, back, last2=True):
                g = it * RING + s
                for q in range(PAIRS):
                    if main:
                        n0 = (g - 1) * PAIRS
                        if q == 0:
                            pe.wait_ge(tr_out, g * NCH)
                        n = n0 + q
                        pe.wait_ge(weff_ready, n + 1)
                        if not (type(n) is int and n < 2):
                            pe.wait_ge(h1_ready, n - 1)
                        for c in range(C1):
                            for r in range(2):
                                t = mm(l1_ps(q % 2, c)[:, r * T:(r + 1) * T], weff[:, q % WR, r, c * P:(c + 1) * P],
                                       histT[:, (s + 1) % 2, 2 * q + r, :], start=True, stop=True)
                        t.then_inc(l1_done, 1)
                    if q == 0 and back:
                        layer2((g - 1) * PAIRS - 1, PAIRS - 1)
                    if q > 0 and main:
                        layer2((g - 1) * PAIRS + q - 1, q - 1)
                    if tr and q < NCH:
                        transpose_chunk(it, s, q)
                    if back and q == 1:
                        scores(g - 2, s)
                    if back and q == 2:
                        pe.wait_ge(mx_ready, g - 1)
                        nc.tensor.transpose(mx_ps, mx[:, :], ident[:, :]).then_inc(mxt_done, 1)
                    if back and q == 3:
                        pe.wait_ge(gmx_ready, g - 1)
                        mm(nmx_ps, gmx[0:1, :], neg1[:, :],
                           start=True, stop=True).then_inc(nmx_done, 1)
                    if back and q == 5:
                        pe.wait_ge(exp_done, g - 1)
                        mm(den_ps, same[:, :], rs[:, :], start=True, stop=True).then_inc(den_done, 1)
                    if back and q == 7:
                        pe.wait_ge(wsum_ready, g - 1)
                        for j in range(J):
                            t = mm(sum_ps, hist[(s + 2) % RING][:, j, :], wsum[:, j, :, :].rearrange("p k b -> p (k b)"),
                                   start=(j == 0), stop=(j == J - 1))
                        t.then_inc(hist_free, 1)

            for s in range(RING):
                step(0, s, True, s >= 1, s >= 2)
            with pe.Fori(1, G // RING) as it:
                for s in range(RING):
                    step(it, s, True, True, True)
            step(G // RING, 0, False, True, True)
            step(G // RING, 1, False, False, True)

            pe.wait_ge(mlp_ready, NMD * 16)
            pe.wait_ge(bn_dve, 1)
            for c in range(4):
                for h in range(2):
                    for k in range(4):
                        kp = E if k == 0 else P
                        t = mm(ps[2 * c + h][:, :], w1m[0:kp, k, c * P:(c + 1) * P], xT[0:kp, k, h * HALF:(h + 1) * HALF],
                               start=(k == 0), stop=(k == 3))
                    t.then_inc(mlp_pe, 1)
            pe.wait_ge(bn_dve, 2)
            for c in range(2):
                for h in range(2):
                    for k in range(4):
                        t = mm(ps[2 * c + h][:, :], w2m[:, k, c * P:(c + 1) * P], y1[:, k, h * HALF:(h + 1) * HALF],
                               start=(k == 0), stop=(k == 3))
                    t.then_inc(mlp_pe, 1)
            pe.wait_ge(bn_dve, 3)
            yv = y2.rearrange("p c (b k) -> p c k b", k=BT)
            for k in range(BT):
                for c in range(2):
                    t = mm(ps[4][:, k * NO:(k + 1) * NO], yv[:, c, k, :], w3m[:, c, :], start=(c == 0), stop=(c == 1))
            t.then_inc(mlp_pe, 1)

        @block.scalar
        def _(act):
            def step(it, s, main, back):
                g = it * RING + s
                ms = (s - 1) % RING
                for q in range(PAIRS):
                    if main:
                        n = (g - 1) * PAIRS + q
                        act.wait_ge(l1_done, n + 1)
                        if not (type(n) is int and n < 2):
                            act.wait_ge(l2_done, n - 1)
                        if q == 0:
                            act.wait_ge(cur_out, g)
                        for c in range(C1):
                            for r in range(2):
                                a = nc.scalar.activation(h1T[:, q % 2, c, r * T:(r + 1) * T],
                                                         l1_ps(q % 2, c)[:, r * T:(r + 1) * T], ACT.Tanh,
                                                         bias=cb_s[:, ms, c, 2 * q + r:2 * q + r + 1], scale=0.5)
                        a.then_inc(h1_ready, 1)
                    if q == 0 and back:
                        tanh2((g - 1) * PAIRS - 1, s, PAIRS - 1)
                    if q > 0 and main:
                        if q == 1 and back and not (type(g) is int and g < 3):
                            act.wait_ge(l3_done, g - 2)
                        tanh2((g - 1) * PAIRS + q - 1, s + 1, q - 1)
                    if back and q == 4:
                        act.wait_ge(nmx_ready, g - 1)
                        nc.scalar.activation(ex[:, :], scm[:, :], ACT.Exp, bias=nmx[:, :],
                                             accum_out=rs[:, :]).then_inc(exp_done, 1)

            def tanh2(n, hs, q):
                act.wait_ge(l2_done, n + 1)
                nc.scalar.activation(h2T[:, hs % 2, :].rearrange("p (j b u) -> p b j u", j=J, u=U)[:, 2 * q:2 * q + 2, :, :],
                                     l2_ps(q % 2)[:, 0:NP].rearrange("p (b j u) -> p b j u", b=2, u=U), ACT.Tanh,
                                     bias=b2f, scale=0.5).then_inc(h2_ready, 1)

            act.wait_ge(setup_dve, 3)
            for s in range(RING):
                step(0, s, s >= 1, s >= 2)
            with act.Fori(1, G // RING) as it:
                for s in range(RING):
                    step(it, s, True, True)
            step(G // RING, 0, True, True)
            step(G // RING, 1, False, True)
            def root(which, n):
                act.wait_ge(var_ready, which + 1)
                nc.scalar.activation(bs[:, 5, 0:n], bs[:, 4, 0:n], ACT.Sqrt).then_inc(root_ready, 1)

            act.wait_ge(mlp_ready, NMD * 16)
            root(0, 4)
            for c in range(4):
                for h in range(2):
                    act.wait_ge(mlp_pe, 2 * c + h + 1)
                    nc.scalar.activation(y1[:, c, h * HALF:(h + 1) * HALF], ps[2 * c + h][:, :], ACT.Identity,
                                         bias=gb1[:, 2, c:c + 1]).then_inc(mlp_act, 1)
            root(1, 4)
            for c in range(2):
                for h in range(2):
                    act.wait_ge(mlp_pe, 8 + 2 * c + h + 1)
                    nc.scalar.activation(y2[:, c, h * HALF:(h + 1) * HALF], ps[2 * c + h][:, :], ACT.Identity,
                                         bias=gb2[:, 2, c:c + 1]).then_inc(mlp_act, 1)
            root(2, 2)

        @block.vector
        def _(dve):
            v = nc.vector
            chain = [0]
            order = setup_dve_chain

            def link(i):
                chain[0] += 1
                i.then_inc(order, 1)
                dve.wait_ge(order, chain[0])

            dve.wait_ge(weights_ready, NWD * 16)
            dve.wait_ge(consts0, 2)
            v.tensor_scalar(w2h[:, :, :], w2[:, :, :], 0.5, None, ALU.mult)
            v.tensor_scalar(w3h[:, :], onesP[:, :], w3[:, 0:1], 0.5, ALU.mult, ALU.mult)
            v.tensor_tensor(wac[:, :], w1[:, 0, :], w1[:, 2, :], ALU.add)
            v.tensor_tensor(wbc[:, :], w1[:, 1, :], w1[:, 2, :], ALU.subtract)
            dve.wait_ge(mask_ready, 16)
            v.tensor_scalar(valid[:, :, :], mraw, 1.0, None, ALU.is_equal)
            link(v.tensor_copy(maskf[:, :, :], mraw))
            v.tensor_scalar(off[:, :, :], valid[:, :, :], -1.0, BIG, ALU.add, ALU.mult)
            v.tensor_reduce(cnt[:, :], maskf[:, :, :], AX.X, ALU.add).then_inc(setup_dve, 1)
            dve.wait_ge(setup_pe, 1)
            for h in range(2):
                xv = xT[:, 1, :].rearrange("p (b k) -> p k b", k=BT)[:, 4 * h:4 * h + 4, :]
                uv = xT[0:E, 0, :].rearrange("p (b k) -> p k b", k=BT)[:, 4 * h:4 * h + 4, :]
                v.tensor_copy(xv, ps[h][:, :].rearrange("p (k b) -> p k b", k=4))
                i = v.tensor_copy(uv, ps[2 + h][0:E, :].rearrange("p (k b) -> p k b", k=4))
            i.then_inc(setup_dve, 1)
            dve.wait_ge(setup_pe, 2)
            link(v.tensor_copy(rcnt[:, :], ps[5][:, 64:64 + G]))
            link(v.reciprocal(rcnt[:, :], rcnt[:, :]))
            v.tensor_tensor(wmean[:, :, :], maskf[:, :, :], rcnt[:, :].unsqueeze(2).broadcast_to([P, G, J]), ALU.mult)
            v.tensor_scalar(b2f, ps[4][:, 0:1], b2v, 0.5, ALU.add, ALU.mult)
            v.tensor_scalar(b3f, ps[5][:, 0:1], b3v, None, ALU.add)
            v.tensor_scalar(vec[:, 6:8], b1v, 0.5, None, ALU.mult).then_inc(order, 1)
            chain[0] += 1
            dve.wait_ge(order, chain[0])
            dve.wait_ge(setup_pe, 3)
            for c in range(C1):
                for h in range(2):
                    i = v.tensor_scalar(cbT[:, c, h * HALF:(h + 1) * HALF], ps[2 * c + h][:, :], 0.5, vec[:, 6 + c:7 + c],
                                        ALU.mult, ALU.add)
            i.then_inc(setup_dve, 1)
            dve.wait_ge(setup_dve, 3)

            def effective(n, cs, q):
                if not (type(n) is int and n < WR):
                    dve.wait_ge(l1_done, n - (WR - 1))
                for r in range(2):
                    i = v.scalar_tensor_tensor(weff[:, q % WR, r, :], w1[:, 3, :], cur_s[:, cs % RING, 2 * q + r:2 * q + r + 1],
                                               wbc[:, :], ALU.mult, ALU.add)
                i.then_inc(weff_ready, 1)

            def step(it, s, tr, main, back, sums):
                g = it * RING + s
                for q in range(PAIRS):
                    if tr and q == 0:
                        if not type(it) is int:
                            dve.wait_ge(h1_ready, (g - RING + 1) * PAIRS)
                        v.tensor_scalar(cur_s[:, s, :], xT[:, 1, bass.ds(g * GB, GB)], 1.0, None, ALU.mult)
                        v.tensor_scalar(cb_s[:, s, :, :], cbT[:, :, bass.ds(g * GB, GB)], 1.0, None,
                                        ALU.mult).then_inc(cur_out, 1)
                        if type(it) is int and s == 0:
                            dve.wait_ge(cur_out, 1)
                            effective(0, 0, 0)
                            effective(1, 0, 1)
                    if main and q < PAIRS - 2:
                        effective((g - 1) * PAIRS + q + 2, s - 1, q + 2)
                    if main and q >= PAIRS - 2 and tr:
                        if q == PAIRS - 2:
                            dve.wait_ge(cur_out, g + 1)
                        effective(g * PAIRS + q - (PAIRS - 2), s, q - (PAIRS - 2))
                    if sums and q == 0:
                        dve.wait_ge(hist_free, RING + g - 2)
                        v.tensor_copy(xT[:, 2:4, bass.ds((g - 3) * GB, GB)],
                                      sum_ps.rearrange("p (k b) -> p k b", k=2)).then_inc(sums_out, 1)
                    if back and q == 1:
                        m = g - 2
                        dve.wait_ge(l3_done, g - 1)
                        v.scalar_tensor_tensor(sc[:, :], s_ps, b3f, valid[:, bass.ds(m, 1), :].rearrange("p a j -> p (a j)"),
                                               ALU.add, ALU.mult).then_inc(biased, 1)
                        dve.wait_ge(biased, g - 1)
                        v.tensor_tensor(scm[:, :], sc[:, :], off[:, bass.ds(m, 1), :].rearrange("p a j -> p (a j)"),
                                        ALU.add).then_inc(masked, 1)
                        dve.wait_ge(masked, g - 1)
                        v.tensor_reduce(mx[:, :], scm[:, :], AX.X, ALU.max).then_inc(mx_ready, 1)
                    if back and q == 3:
                        dve.wait_ge(mxt_done, g - 1)
                        v.tensor_reduce(gmx[:, :].rearrange("p (b u) -> p b u", u=U),
                                        mx_ps.rearrange("p (b u) -> p b u", u=U).unsqueeze(2).broadcast_to([1, GB, U, U]), AX.X,
                                        ALU.max).then_inc(gmx_ready, 1)
                    if back and q == 4:
                        dve.wait_ge(nmx_done, g - 1)
                        v.tensor_copy(nmx[:, :], nmx_ps).then_inc(nmx_ready, 1)
                        v.tensor_tensor(wsum[:, :, 1, :],
                                        wmean[:, bass.ds(g - 2, 1), :].rearrange("p a j -> p (a j)").unsqueeze(2).broadcast_to([P, J, GB]),
                                        blk[:, :].unsqueeze(1).broadcast_to([P, J, GB]), ALU.mult)
                    if back and q == 6:
                        dve.wait_ge(den_done, g - 1)
                        v.reciprocal(rden[:, :], den_ps).then_inc(rden_ready, 1)
                        dve.wait_ge(rden_ready, g - 1)
                        v.scalar_tensor_tensor(pr[:, :], ex[:, :], rden[:, 0:1],
                                               maskf[:, bass.ds(g - 2, 1), :].rearrange("p a j -> p (a j)"),
                                               ALU.mult, ALU.mult).then_inc(pr_ready, 1)
                        dve.wait_ge(pr_ready, g - 1)
                        v.tensor_tensor(wsum[:, :, 0, :], pr[:, :].unsqueeze(2).broadcast_to([P, J, GB]),
                                        blk[:, :].unsqueeze(1).broadcast_to([P, J, GB]), ALU.mult).then_inc(wsum_ready, 1)
                    if tr and q < NCH:
                        for k in [q]:
                            dve.wait_ge(tr_done, g * NCH + (k + 1))
                            if k == 0 and not (type(g) is int and g < 2):
                                dve.wait_ge(l1_done, (g - 1) * PAIRS)
                            j0, nj = CHUNKS[k]
                            dst = histT[:, s % 2, :, :].rearrange("p b (j u) -> p j b u", u=U)[:, j0:j0 + nj, :, :]
                            src = tr_ps[:, 0:nj * P].rearrange("p (j b u) -> p j b u", j=nj, u=U)
                            v.tensor_copy(dst, src).then_inc(tr_out, 1)

            for s in range(RING):
                step(0, s, True, s >= 1, s >= 2, s >= 3)
            with dve.Fori(1, G // RING) as it:
                for s in range(RING):
                    step(it, s, True, True, True, True)
            step(G // RING, 0, False, True, True, True)
            step(G // RING, 1, False, False, True, True)
            dve.wait_ge(hist_free, RING + G)
            link(v.tensor_copy(xT[:, 2:4, (G - 1) * GB:G * GB], sum_ps.rearrange("p (k b) -> p k b", k=2)))

            def norm_scale(which, x, parts, gb):
                n = len(parts)
                link(v.memset(mv[:, :, :], 1.0))
                for c, kp in enumerate(parts):
                    for h in range(2):
                        i = v.bn_stats(st[0:kp, c, h, :], x[0:kp, c, h * HALF:(h + 1) * HALF])
                link(i)
                for c, kp in enumerate(parts):
                    i = v.bn_aggr(mv[0:kp, c, :], st[0:kp, c, :, :].rearrange("p h s -> p (h s)"))
                link(i)
                v.tensor_scalar(bs[:, 4, 0:n], mv[:, 0:n, 1], EPS, None, ALU.add).then_inc(var_ready, 1)
                dve.wait_ge(root_ready, which + 1)
                link(v.reciprocal(bs[:, 0, 0:n], bs[:, 5, 0:n]))
                link(v.tensor_tensor(bs[:, 6, 0:n], bs[:, 0, 0:n], bs[:, 0, 0:n], ALU.mult))
                link(v.tensor_tensor(bs[:, 6, 0:n], bs[:, 6, 0:n], bs[:, 4, 0:n], ALU.mult))
                link(v.tensor_scalar(bs[:, 6, 0:n], bs[:, 6, 0:n], -0.5, 1.5, ALU.mult, ALU.add))
                link(v.tensor_tensor(bs[:, 0, 0:n], bs[:, 0, 0:n], bs[:, 6, 0:n], ALU.mult))
                link(v.tensor_tensor(bs[:, 1, 0:n], bs[:, 0, 0:n], gb[:, 0, 0:n], ALU.mult))
                link(v.tensor_tensor(bs[:, 2, 0:n], mv[:, 0:n, 0], bs[:, 1, 0:n], ALU.mult))
                link(v.tensor_tensor(bs[:, 3, 0:n], gb[:, 1, 0:n], bs[:, 2, 0:n], ALU.subtract))

            dve.wait_ge(mlp_ready, NMD * 16)
            link(v.memset(gb0[E:P, :, 0:1], 1.0))
            norm_scale(0, xT, [E, P, P, P], gb0)
            for c, kp in enumerate([E, P, P, P]):
                i = v.tensor_scalar(xT[0:kp, c, :], xT[0:kp, c, :], bs[0:kp, 1, c:c + 1], bs[0:kp, 3, c:c + 1],
                                    ALU.mult, ALU.add)
            i.then_inc(bn_dve, 1)
            for which, (y, n, got, gb) in enumerate(((y1, 4, 8, gb1), (y2, 2, 12, gb2)), 1):
                dve.wait_ge(mlp_act, got)
                norm_scale(which, y, [P] * n, gb)
                for c in range(n):
                    i = v.tensor_scalar(y[:, c, :], y[:, c, :], bs[:, 1, c:c + 1], bs[:, 3, c:c + 1], ALU.mult, ALU.add)
                link(i)
                for c in range(n):
                    i = v.scalar_tensor_tensor(y[:, c, :], y[:, c, :], 0.1, y[:, c, :], ALU.mult, ALU.max)
                i.then_inc(bn_dve, 1)
            dve.wait_ge(mlp_pe, 13)
            v.tensor_tensor(outs[:, :, :], ps[4][:, 0:BT * NO].rearrange("p (k n) -> p k n", n=NO),
                            b3m[:, :].unsqueeze(1).broadcast_to([P, BT, NO]), ALU.add).then_inc(out_ready, 1)


_INS=["r_uid","r_mid","r_cat","r_historical_mid","r_historical_cat","r_mask"]+["L0_rec_"+x for x in "user_table mat_table cat_table lau_w1 lau_b1 lau_w2 lau_b2 lau_w3 lau_b3 bn0_g bn0_b mlp_w1 mlp_b1 bn1_g bn1_b mlp_w2 mlp_b2 bn2_g bn2_b mlp_w3 mlp_b3".split()]
def kernel(**inputs):
    import numpy as _np
    import concourse.bacc as _bacc
    from concourse import mybir as _mybir
    from concourse.bass_utils import run_bass_kernel_spmd as _run
    nc = _bacc.Bacc("TRN2", target_bir_lowering=False, num_devices=1)
    arrays, aps = {}, {}
    for name in _INS:
        a = _np.ascontiguousarray(inputs[name])
        arrays[f"in_{name}_dram"] = a
        aps[name]=nc.dram_tensor(f"in_{name}_dram", a.shape, _mybir.dt.from_np(a.dtype), kind="ExternalInput").ap()
    out = nc.dram_tensor("out_0_dram", (1024,2), _mybir.dt.float32, kind="ExternalOutput").ap()
    build(nc, aps, out)
    r = _run(nc, [arrays], core_ids=[0])
    return r.results[0]["out_0_dram"]
```

```python
from contextlib import ExitStack

import concourse.bass as bass
from concourse import mybir

F32 = mybir.dt.float32
I32 = mybir.dt.int32
F16 = mybir.dt.float16
BF16 = mybir.dt.bfloat16
ALU = mybir.AluOpType
ACT = mybir.ActivationFunctionType
AX = mybir.AxisListType

P = 128
B, T, E = 1024, 200, 64
F = 2 * E
GB = 16
U = P // GB
J = T // U
G = B // GB
RING = 4
NP = 2 * T
H1, H2 = 256, 128
C1 = H1 // P
WR = 4
PAIRS = GB // 2
K = 13
QUAD = 4
QUADS = [(j, min(QUAD, K - j)) for j in range(0, K, QUAD)]
CAT_AT = {1 + n: (j // QUAD, j, min(2, K - j)) for n, j in enumerate(range(0, K, 2))}
QUAD_AT = {2 * i: i for i in range(len(QUADS))}
PLAIN = [(j, min(QUAD, J - j)) for j in range(K, J, QUAD)]
TR_AT = {4: [QUADS[0], PLAIN[0]], 5: [QUADS[1], PLAIN[1]], 6: PLAIN[2:], 7: QUADS[2:3]}
TR_LAST = QUADS[3]
SUM_FROM = 6
SUM_KEPT = 9
TR_ORDER = [chunk for q in sorted(TR_AT) for chunk in TR_AT[q]] + [TR_LAST]
NCH = len(TR_ORDER)
BT = B // P
M1, M2, NO = 512, 256, 2
DX = 7 * E
EPS = 1e-5
NCAT = 1000
NC = -(-NCAT // P)
BIG = 2.0 ** 31
HALF = 512


def build(nc, ins, out):
    with ExitStack() as ctx:
        def sb(name, shape, dt=F32):
            return ctx.enter_context(nc.sbuf_tensor(name, shape, dt))

        def sem(name):
            return ctx.enter_context(nc.semaphore(name))

        w = {k[len("L0_rec_"):]: v for k, v in ins.items() if k.startswith("L0_rec_")}

        idx = sb("idx", [P, RING, 2, J], I32)
        hist = [sb(f"hist{s}", [P, J, F]) for s in range(RING)]
        histT = sb("histT", [P, 2, GB, T])
        h1f = sb("h1f", [P, C1, NP])
        h1T = sb("h1T", [P, 2, C1, 2, NP], F16)
        h2f = sb("h2f", [P, 2, NP])
        h2T = sb("h2T", [P, 2, 2, GB * T], F16)
        onehot = sb("onehot", [P, 2, NC, QUAD * P], BF16)
        catrow = sb("catrow", [P, QUAD * P], F16)
        catf = sb("catf", [P, K], F16)
        table = sb("table", [P, NC, 3, E], BF16)
        catid = sb("catid", [P, NC])
        cati = sb("cati", [P, NC], I32)
        identh = sb("identh", [P, P], F16)
        weff = sb("weff", [P, WR, 2, H1])
        wsum = sb("wsum", [P, J, 2, GB])
        xT = sb("xT", [P, 4, B])
        cbT = sb("cbT", [P, C1, B])
        cur_s = sb("cur_s", [P, RING, GB])
        cb_s = sb("cb_s", [P, RING, C1, GB])
        valid = sb("valid", [P, G, J])
        off = sb("off", [P, G, J])
        mraw = off[:, :, :].bitcast(I32)
        maskf = sb("maskf", [P, G, J])
        wmean = sb("wmean", [P, G, J])
        w1 = sb("w1", [P, 4, H1])
        wac = sb("wac", [P, H1])
        wbc = sb("wbc", [P, H1])
        w2 = sb("w2", [P, C1, H2])
        w2h = sb("w2h", [P, C1, H2])
        w2p = sb("w2p", [P, C1, 2, H2], F16)
        w3 = sb("w3", [P, 1])
        w3p = sb("w3p", [P, 3], BF16)
        w3r = sb("w3r", [P, 1])
        vec = sb("vec", [P, 8])
        b1v, b2v, b3v = vec[:, 0:2], vec[:, 2:3], vec[:, 3:4]
        b2f, b3f = vec[:, 4:5], vec[:, 5:6]
        onesP = sb("onesP", [P, P])
        neg1 = sb("neg1", [1, 1])
        ident = sb("ident", [P, P])
        same = sb("same", [P, P])
        blk = sb("blk", [P, GB])
        cidx = sb("cidx", [P, 3, BT], I32)
        cnt = sb("cnt", [P, G])
        rcnt = sb("rcnt", [P, G])
        s3 = sb("s3", [P, J])
        sc = sb("sc", [P, J])
        gm = sb("gm", [1, GB])
        scm = sb("scm", [P, J])
        ex = sb("ex", [P, J])
        pr = sb("pr", [P, J])
        mx = sb("mx", [P, 1])
        gmx = sb("gmx", [1, P])
        nmx = sb("nmx", [P, 1])
        rs = sb("rs", [P, 1])
        rden = sb("rden", [P, GB])
        rsb = sb("rsb", [P, GB])
        w3m = sb("w3m", [P, M2 // P, NO])
        gb0 = sb("gb0", [P, 2, 4])
        gb1 = sb("gb1", [P, 3, M1 // P])
        gb2 = sb("gb2", [P, 3, M2 // P])
        b3m = sb("b3m", [P, NO])
        st = sb("st", [P, 4, 2, 6])
        mv = sb("mv", [P, 4, 2])
        bs = sb("bs", [P, 7, 4])
        outs = sb("outs", [P, BT, NO])
        w3h = h1f[:, 0, 0:P]
        h2w = h2T[:, :, :, :].rearrange("p s a n -> p (s a n)").bitcast(F32)
        W0 = GB * T
        curg = h2w[:, W0:W0 + BT * F].rearrange("p (k f) -> p k f", k=BT)
        userg = h2w[:, W0 + BT * F:W0 + BT * (F + E)].rearrange("p (k f) -> p k f", k=BT)
        tabf = histT[:, 1, :, :].rearrange("p b n -> p (b n)")[:, 0:NC * E].rearrange("p (c e) -> p c e", c=NC)
        mlpw = onehot[:, :, :, :].rearrange("p a c n -> p (a c n)").bitcast(F32)
        w1m = mlpw[:, 0:4 * M1].rearrange("p (c n) -> p c n", c=4)
        w2m = mlpw[:, 4 * M1:4 * M1 + (M1 // P) * M2].rearrange("p (c n) -> p c n", n=M2)
        y1 = h2w[:, 0:4 * B].rearrange("p (c n) -> p c n", c=4)
        y2 = histT[:, :, :, :].rearrange("p a b n -> p (a b n)")[:, 0:2 * B].rearrange("p (c n) -> p c n", c=2)

        ps = [ctx.enter_context(nc.psum_tensor(f"ps{i}", [P, 512], F32)) for i in range(8)]
        l1_ps = ps[0:2]
        l2_ps = ps[2]
        tr_ps = ps[3:5]
        row_ps = ps[6]
        cat_ps = ps[7]
        s_ps = ps[5][:, 0:3 * J]
        nmx_ps = ps[5][:, 75:76]
        den_ps = ps[5][:, 80:96]
        sum_ps = ps[5][:, 96:128]
        mx_ps = ps[5][0:1, P:2 * P]

        gathered = [sem(f"gathered{s}") for s in range(RING)]
        idx_ready = [sem(f"idx_ready{s}") for s in range(RING)]
        hist_free = sem("hist_free")
        gather_begun = sem("gather_begun")
        load_begun = sem("load_begun")
        weights_ready = sem("weights_ready")
        mlp_ready = sem("mlp_ready")
        mask_ready = sem("mask_ready")
        table_ready = sem("table_ready")
        cidx_ready = sem("cidx_ready")
        cur_ready = sem("cur_ready")
        consts0 = sem("consts0")
        consts = sem("consts")
        setup_dve = sem("setup_dve")
        setup_pe = sem("setup_pe")
        tr_done = sem("tr_done")
        tr_out = sem("tr_out")
        catf_ready = sem("catf_ready")
        row_done = sem("row_done")
        row_out = sem("row_out")
        onehot_ready = sem("onehot_ready")
        cat_done = sem("cat_done")
        cat_out = sem("cat_out")
        cur_out = sem("cur_out")
        weff_ready = sem("weff_ready")
        l1_done = sem("l1_done")
        h1_ready = sem("h1_ready")
        h1_split = sem("h1_split")
        l2_done = sem("l2_done")
        h2_ready = sem("h2_ready")
        h2_split = sem("h2_split")
        l3_done = sem("l3_done")
        parts_added = sem("parts_added")
        biased = sem("biased")
        masked = sem("masked")
        mx_ready = sem("mx_ready")
        mxt_done = sem("mxt_done")
        gm_ready = sem("gm_ready")
        gmx_ready = sem("gmx_ready")
        nmx_done = sem("nmx_done")
        nmx_ready = sem("nmx_ready")
        exp_done = sem("exp_done")
        rsb_ready = sem("rsb_ready")
        rden_ready = sem("rden_ready")
        pr_ready = sem("pr_ready")
        wsum_ready = sem("wsum_ready")
        sums_out = sem("sums_out")
        bn_dve = sem("bn_dve")
        mlp_pe = sem("mlp_pe")
        mlp_act = sem("mlp_act")
        out_ready = sem("out_ready")
        var_ready = sem("var_ready")
        root_ready = sem("root_ready")
        stored = sem("stored")
        setup_dve_chain = sem("dve_chain")

        mid_v = ins["r_historical_mid"].rearrange("b (u j) -> (b u) j", u=U)
        cat_v = ins["r_historical_cat"].rearrange("b (u j) -> (b u) j", u=U)
        mask_v = ins["r_mask"].rearrange("(g b) (u j) -> (b u) g j", g=G, u=U)

        def columns(half, q):
            return half.rearrange("p (j b u) -> p b j u", j=J, u=U)[:, 2 * q:2 * q + 2, :, :]

        NCAT2 = len(CAT_AT)
        NG = 2 * J - K
        NWD = 6
        NMD = 15

        block = ctx.enter_context(nc.Block())

        @block.sync
        def _(sp):
            for k, n in enumerate(("r_mid", "r_cat", "r_uid")):
                sp.dma_start(cidx[:, k, :], ins[n].rearrange("(p k) -> p k", k=BT)).then_inc(cidx_ready, 16)
            for s in range(RING):
                sp.dma_start(idx[:, s, 0, :], mid_v[s * P:(s + 1) * P, :]).then_inc(idx_ready[s], 16)
                sp.dma_start(idx[:, s, 1, :], cat_v[s * P:(s + 1) * P, :]).then_inc(idx_ready[s], 16)
            sp.dma_start(w1[:, :, :], w["lau_w1"].rearrange("(c p) n -> p c n", p=P)).then_inc(weights_ready, 16)
            sp.dma_start(w2[:, :, :], w["lau_w2"].rearrange("(c p) n -> p c n", p=P)).then_inc(weights_ready, 16)
            sp.dma_start(w3[:, :], w["lau_w3"]).then_inc(weights_ready, 16)
            sp.dma_start(b1v, w["lau_b1"].rearrange("(c p) -> p c", p=P), allow_slow_non_contiguous=True).then_inc(weights_ready, 16)
            sp.dma_start(b2v, w["lau_b2"].rearrange("(p a) -> p a", a=1)).then_inc(weights_ready, 16)
            sp.dma_start(b3v, w["lau_b3"].rearrange("(a n) -> a n", a=1).broadcast_to([P, 1])).then_inc(weights_ready, 16)
            full = NCAT // P * P
            sp.dma_start(tabf[:, 0:NC - 1, :], w["cat_table"][0:full, :].rearrange("(c p) e -> p c e", p=P)).then_inc(table_ready, 16)
            sp.dma_start(tabf[0:NCAT - full, NC - 1, :], w["cat_table"][full:NCAT, :]).then_inc(table_ready, 16)
            sp.dma_start(mraw, mask_v).then_inc(mask_ready, 16)
            sp.dma_start(w3m[:, :, :], w["mlp_w3"].rearrange("(c p) n -> p c n", p=P)).then_inc(mlp_ready, 16)
            for k, n in enumerate(("bn0_g", "bn0_b")):
                sp.dma_start(gb0[0:E, k, 0:1], w[n][0:E].rearrange("(p a) -> p a", a=1)).then_inc(mlp_ready, 16)
                sp.dma_start(gb0[:, k, 1:4], w[n][E:DX].rearrange("(c p) -> p c", p=P), allow_slow_non_contiguous=True).then_inc(mlp_ready, 16)
            for k, n in enumerate(("bn1_g", "bn1_b", "mlp_b1")):
                sp.dma_start(gb1[:, k, :], w[n].rearrange("(c p) -> p c", p=P), allow_slow_non_contiguous=True).then_inc(mlp_ready, 16)
            for k, n in enumerate(("bn2_g", "bn2_b", "mlp_b2")):
                sp.dma_start(gb2[:, k, :], w[n].rearrange("(c p) -> p c", p=P), allow_slow_non_contiguous=True).then_inc(mlp_ready, 16)
            sp.dma_start(b3m[:, :], w["mlp_b3"].rearrange("(a n) -> a n", a=1).broadcast_to([P, NO])).then_inc(mlp_ready, 16)
            with sp.Fori(1, G // RING) as it:
                for s in range(RING):
                    sp.wait_ge(gathered[s], it * (NG * 16))
                    sp.sem_inc(load_begun, 1)
                    sp.wait_ge(catf_ready, it * RING + (s - RING + 1))
                    row = it * (RING * P) + s * P
                    sp.dma_start(idx[:, s, 0, :], mid_v[bass.ds(row, P), :]).then_inc(idx_ready[s], 16)
                    sp.dma_start(idx[:, s, 1, :], cat_v[bass.ds(row, P), :]).then_inc(idx_ready[s], 16)
            sp.wait_ge(cat_done, G * NCAT2)
            sp.dma_start(w1m[0:E, 0, :], w["mlp_w1"][0:E, :]).then_inc(mlp_ready, 16)
            sp.dma_start(w1m[:, 1:4, :], w["mlp_w1"][E:DX, :].rearrange("(c p) n -> p c n", p=P)).then_inc(mlp_ready, 16)
            sp.dma_start(w2m[:, :, :], w["mlp_w2"].rearrange("(c p) n -> p c n", p=P)).then_inc(mlp_ready, 16)
            sp.wait_ge(out_ready, 1)
            sp.dma_start(out.rearrange("(p k) n -> p k n", k=BT), outs[:, :, :]).then_inc(stored, 16)
            sp.wait_ge(stored, 16)

        @block.gpsimd
        def _(pool):
            def gather(dst, table, col, done):
                nc.gpsimd.indirect_dma_start(out=dst, out_offset=None, in_=table,
                                             in_offset=bass.IndirectOffsetOnAxis(ap=col, axis=0)).then_inc(done, 16)

            nc.gpsimd.memset(onesP[:, :], 1.0).then_inc(consts0, 1)
            nc.gpsimd.memset(neg1[:, :], -1.0).then_inc(consts0, 1)
            nc.gpsimd.iota(cati[:, :], pattern=[[P, NC]], base=0, channel_multiplier=1).then_inc(consts, 1)
            pool.wait_ge(cidx_ready, 48)
            for k in range(BT):
                gather(curg[:, k, 0:E], w["mat_table"], cidx[:, 0, k:k + 1], cur_ready)
                gather(curg[:, k, E:F], w["cat_table"], cidx[:, 1, k:k + 1], cur_ready)
                gather(userg[:, k, :], w["user_table"], cidx[:, 2, k:k + 1], cur_ready)
            pool.wait_ge(consts0, 2)
            nc.gpsimd.affine_select(out=ident[:, :], in_=onesP[:, :], compare_op=ALU.is_equal, fill=0.0, base=0,
                                    pattern=[[-1, P]], channel_multiplier=1).then_inc(consts0, 1)
            sv = same[:, :].rearrange("p (b u) -> p b u", u=U)
            ov = onesP[:, :].rearrange("p (b u) -> p b u", u=U)
            nc.gpsimd.affine_select(out=sv, in_=ov, compare_op=ALU.is_ge, fill=0.0, base=0,
                                    pattern=[[-U, GB], [0, U]], channel_multiplier=1).then_inc(consts0, 1)
            nc.gpsimd.affine_select(out=blk[:, :], in_=onesP[:, 0:GB], compare_op=ALU.is_ge, fill=0.0, base=0,
                                    pattern=[[-U, GB]], channel_multiplier=1).then_inc(consts0, 1)
            pool.wait_ge(consts0, 5)
            nc.gpsimd.affine_select(out=sv, in_=sv, compare_op=ALU.is_ge, fill=0.0, base=U - 1,
                                    pattern=[[U, GB], [0, U]], channel_multiplier=-1).then_inc(consts, 1)
            nc.gpsimd.affine_select(out=blk[:, :], in_=blk[:, :], compare_op=ALU.is_ge, fill=0.0, base=U - 1,
                                    pattern=[[U, GB]], channel_multiplier=-1).then_inc(consts, 1)

            with pool.Fori(0, G // RING) as it:
                for s in range(RING):
                    pool.wait_ge(idx_ready[s], it * 32 + 32)
                    pool.wait_ge(hist_free, it * RING + (s + 1))
                    pool.sem_inc(gather_begun, 1)
                    for j in range(J):
                        gather(hist[s][:, j, 0:E], w["mat_table"], idx[:, s, 0, j:j + 1], gathered[s])
                        if j >= K:
                            gather(hist[s][:, j, E:F], w["cat_table"], idx[:, s, 1, j:j + 1], gathered[s])

        @block.tensor
        def _(pe):
            mm = nc.tensor.matmul
            pe.sem_inc(hist_free, RING)

            pe.wait_ge(cur_ready, 3 * BT * 16)
            pe.wait_ge(consts0, 5)
            for k in range(BT):
                nc.tensor.transpose(ps[k // 4][:, (k % 4) * P:(k % 4 + 1) * P], curg[:, k, :], ident[:, :])
                t = nc.tensor.transpose(ps[2 + k // 4][0:E, (k % 4) * P:(k % 4 + 1) * P], userg[:, k, :], ident[:, :])
            t.then_inc(setup_pe, 1)
            pe.wait_ge(setup_dve, 1)
            for c in range(C1):
                mm(ps[4][:, 0:1], w2h[:, c, :], onesP[:, 0:1], start=(c == 0), stop=(c == C1 - 1))
            mm(ps[5][:, 0:1], w3h[:, :], onesP[:, 0:1], start=True, stop=True)
            pe.wait_ge(consts, 3)
            mm(ps[5][:, 64:64 + G], same[:, :], cnt[:, :], start=True, stop=True).then_inc(setup_pe, 1)
            pe.wait_ge(setup_dve, 2)
            for c in range(C1):
                for h in range(2):
                    t = mm(ps[2 * c + h][:, :], wac[:, c * P:(c + 1) * P], xT[:, 1, h * HALF:(h + 1) * HALF],
                           start=True, stop=True)
            t.then_inc(setup_pe, 1)
            pe.wait_ge(setup_dve, 3)

            def transpose_chunk(it, s, chunk):
                g = it * RING + s
                k = TR_ORDER.index(chunk)
                n = g * NCH + k
                if k == 0:
                    pe.wait_ge(gathered[s], it * (NG * 16) + NG * 16)
                if not (type(n) is int and n < 2):
                    pe.wait_ge(tr_out, n - 1)
                j0, nj = chunk
                if j0 < K:
                    pe.wait_ge(cat_out, g * NCAT2 + (j0 + nj + 1) // 2)
                for j in range(nj):
                    t = nc.tensor.transpose(tr_ps[(s * NCH + k) % 2][:, j * P:(j + 1) * P], hist[s][:, j0 + j, :], ident[:, :])
                t.then_inc(tr_done, 1)

            def spread_categories(g, i):
                if i == 0:
                    pe.wait_ge(catf_ready, g + 1)
                n = g * len(QUADS) + i
                if not (type(n) is int and n < 1):
                    pe.wait_ge(row_out, n)
                j0, nj = QUADS[i]
                for j in range(nj):
                    t = mm(row_ps[:, j * P:(j + 1) * P], catf[:, j0 + j:j0 + j + 1].broadcast_to([P, P]), identh[:, :],
                           start=True, stop=True)
                t.then_inc(row_done, 1)

            def category_rows(g, s, q, between):
                i, j0, nj = CAT_AT[q]
                n = g * NCAT2 + j0 // 2
                pe.wait_ge(onehot_ready, g * len(QUADS) + (i + 1))
                if not (type(n) is int and n < 1):
                    pe.wait_ge(cat_out, n)
                slot = (s * len(QUADS) + i) % 2
                for j in range(nj):
                    col = (j0 + j - i * QUAD) * P
                    for c in range(NC):
                        t = mm(cat_ps[:, j * 3 * E:(j + 1) * 3 * E], onehot[:, slot, c, col:col + P],
                               table[:, c, :, :].rearrange("p s e -> p (s e)"), start=(c == 0), stop=(c == NC - 1))
                        if c % 4 == 3 and c < NC - 1:
                            between(q)
                t.then_inc(cat_done, 1)

            def layer2(n, q, at, between):
                pe.wait_ge(h1_split, n * 2 + 2)
                if not (type(n) is int and n < 1):
                    pe.wait_ge(h2_ready, n)
                for c in range(C1):
                    for wp, hp in ((0, 0), (0, 1), (1, 0)):
                        t = mm(l2_ps[:, 0:NP], w2p[:, c, wp, :], h1T[:, q % 2, c, hp, :], start=(c + wp + hp == 0),
                               stop=(c * wp == 1))
                    if c == 0:
                        between(at)
                t.then_inc(l2_done, 1)
                between(at)

            def scores(b, bs_):
                pe.wait_ge(h2_split, b * PAIRS + PAIRS)
                if not (type(b) is int and b < 1):
                    pe.wait_ge(sums_out, b)
                for j in range(J):
                    for part in range(2):
                        t = mm(s_ps[:, 3 * j:3 * j + 3], h2T[:, bs_ % 2, part, j * P:(j + 1) * P], w3p[:, :],
                               start=(part == 0), stop=(part == 1))
                t.then_inc(l3_done, 1)

            def sum_tile(g, s, j):
                if j == 0:
                    pe.wait_ge(wsum_ready, g - 1)
                t = mm(sum_ps, hist[(s + 2) % RING][:, j, :], wsum[:, j, :, :].rearrange("p k b -> p (k b)"),
                       start=(j == 0), stop=(j == J - 1), skip_group_check=True)
                if j == J - 1:
                    pe.wait_ge(rsb_ready, g - 1)
                    mm(den_ps, onesP[:, :], rsb[:, :], start=True, stop=True, skip_group_check=True).then_inc(hist_free, 1)

            def step(it, s, tr, main, back):
                g = it * RING + s
                tiles = list(range(J))

                def between(q, n=1):
                    if back and q >= SUM_FROM and (n > 1 or len(tiles) > SUM_KEPT):
                        for j in tiles[:n]:
                            sum_tile(g, s, j)
                        del tiles[:n]

                for q in range(PAIRS):
                    if tr and q in QUAD_AT:
                        spread_categories(g, QUAD_AT[q])
                    if main:
                        n = (g - 1) * PAIRS + q
                        if q == 0:
                            pe.wait_ge(tr_out, g * NCH)
                        pe.wait_ge(weff_ready, n + 1)
                        for c in range(C1):
                            if not (type(n) is int and n < 1):
                                pe.wait_ge(h1_ready, n * 2 + (c - 1))
                            for r in range(2):
                                t = mm(l1_ps[c][:, r * T:(r + 1) * T], weff[:, q % WR, r, c * P:(c + 1) * P],
                                       histT[:, (s + 1) % 2, 2 * q + r, :], start=True, stop=True)
                                if r == 0:
                                    between(q)
                            t.then_inc(l1_done, 1)
                            between(q)
                    if q == 0 and back:
                        layer2((g - 1) * PAIRS - 1, PAIRS - 1, q, between)
                    if tr and q == PAIRS - 1:
                        for chunk in TR_AT[q]:
                            transpose_chunk(it, s, chunk)
                        category_rows(g, s, q, between)
                    if q > 0 and main:
                        layer2((g - 1) * PAIRS + q - 1, q - 1, q, between)
                    if back and q == 2:
                        scores(g - 2, s)
                    if tr and q in CAT_AT and q < PAIRS - 1:
                        category_rows(g, s, q, between)
                    if back and q == 3:
                        pe.wait_ge(mx_ready, g - 1)
                        nc.tensor.transpose(mx_ps, mx[:, :], ident[:, :]).then_inc(mxt_done, 1)
                    if back and q == 4:
                        pe.wait_ge(gmx_ready, g - 1)
                        mm(nmx_ps, gmx[0:1, :], neg1[:, :], start=True, stop=True).then_inc(nmx_done, 1)
                    if tr and q in TR_AT and q < PAIRS - 1:
                        for chunk in TR_AT[q]:
                            transpose_chunk(it, s, chunk)
                    if q == PAIRS - 1:
                        between(q, 2)
                        if tr:
                            transpose_chunk(it, s, TR_LAST)
                        between(q, J)

            for s in range(RING):
                step(0, s, True, s >= 1, s >= 2)
            with pe.Fori(1, G // RING) as it:
                for s in range(RING):
                    step(it, s, True, True, True)
            step(G // RING, 0, False, True, True)
            step(G // RING, 1, False, False, True)

            pe.wait_ge(mlp_ready, NMD * 16)
            pe.wait_ge(bn_dve, 1)
            for c in range(4):
                for h in range(2):
                    for k in range(4):
                        kp = E if k == 0 else P
                        t = mm(ps[2 * c + h][:, :], w1m[0:kp, k, c * P:(c + 1) * P], xT[0:kp, k, h * HALF:(h + 1) * HALF],
                               start=(k == 0), stop=(k == 3))
                    t.then_inc(mlp_pe, 1)
            pe.wait_ge(bn_dve, 2)
            for c in range(2):
                for h in range(2):
                    for k in range(4):
                        t = mm(ps[2 * c + h][:, :], w2m[:, k, c * P:(c + 1) * P], y1[:, k, h * HALF:(h + 1) * HALF],
                               start=(k == 0), stop=(k == 3))
                    t.then_inc(mlp_pe, 1)
            pe.wait_ge(bn_dve, 3)
            yv = y2.rearrange("p c (b k) -> p c k b", k=BT)
            for k in range(BT):
                for c in range(2):
                    t = mm(ps[4][:, k * NO:(k + 1) * NO], yv[:, c, k, :], w3m[:, c, :], start=(c == 0), stop=(c == 1))
            t.then_inc(mlp_pe, 1)

        @block.scalar
        def _(act):
            def step(it, s, tr, main, back):
                g = it * RING + s
                ms = (s - 1) % RING
                for q in range(PAIRS):
                    if tr and q in QUAD_AT:
                        row_copy(g, QUAD_AT[q])
                    if main:
                        n = (g - 1) * PAIRS + q
                        if q == 0:
                            act.wait_ge(cur_out, g)
                        if not (type(n) is int and n < 2):
                            act.wait_ge(l2_done, n - 1)
                        for c in range(C1):
                            act.wait_ge(l1_done, n * 2 + (c + 1))
                            if not (type(n) is int and n < 1):
                                act.wait_ge(h1_split, n * 2 + (c - 1))
                            for dst in (h1f[:, c, :], h1T[:, q % 2, c, 0, :]):
                                for r in range(2):
                                    a = nc.scalar.activation(dst[:, r * T:(r + 1) * T],
                                                             l1_ps[c][:, r * T:(r + 1) * T], ACT.Tanh,
                                                             bias=cb_s[:, ms, c, 2 * q + r:2 * q + r + 1], scale=0.5)
                            a.then_inc(h1_ready, 1)
                    if q == 0 and back:
                        tanh2((g - 1) * PAIRS - 1, s, PAIRS - 1)
                    if back and q == 5:
                        act.wait_ge(nmx_ready, g - 1)
                        nc.scalar.activation(ex[:, :], scm[:, :], ACT.Exp, bias=nmx[:, :],
                                             accum_out=rs[:, :]).then_inc(exp_done, 1)
                    if q > 0 and main:
                        if q == 1 and back and not (type(g) is int and g < 3):
                            act.wait_ge(l3_done, g - 2)
                        tanh2((g - 1) * PAIRS + q - 1, s + 1, q - 1)

            def row_copy(g, i):
                n = g * len(QUADS) + i
                nj = QUADS[i][1]
                act.wait_ge(row_done, n + 1)
                if not (type(n) is int and n < 1):
                    act.wait_ge(onehot_ready, n)
                nc.scalar.activation(catrow[:, 0:nj * P], row_ps[:, 0:nj * P], ACT.Identity).then_inc(row_out, 1)

            def tanh2(n, hs, q):
                act.wait_ge(l2_done, n + 1)
                if not (type(n) is int and n < 2):
                    act.wait_ge(h2_split, n - 1)
                nc.scalar.activation(h2f[:, q % 2, :], l2_ps[:, 0:NP], ACT.Tanh, bias=b2f, scale=0.5)
                nc.scalar.activation(columns(h2T[:, hs % 2, 0, :], q), l2_ps[:, 0:NP].rearrange("p (b j u) -> p b j u", b=2, u=U),
                                     ACT.Tanh, bias=b2f, scale=0.5).then_inc(h2_ready, 1)

            act.wait_ge(setup_dve, 3)
            for s in range(RING):
                step(0, s, True, s >= 1, s >= 2)
            with act.Fori(1, G // RING) as it:
                for s in range(RING):
                    step(it, s, True, True, True)
            step(G // RING, 0, False, True, True)
            step(G // RING, 1, False, False, True)
            def root(which, n):
                act.wait_ge(var_ready, which + 1)
                nc.scalar.activation(bs[:, 5, 0:n], bs[:, 4, 0:n], ACT.Sqrt).then_inc(root_ready, 1)

            act.wait_ge(mlp_ready, NMD * 16)
            root(0, 4)
            for c in range(4):
                for h in range(2):
                    act.wait_ge(mlp_pe, 2 * c + h + 1)
                    nc.scalar.activation(y1[:, c, h * HALF:(h + 1) * HALF], ps[2 * c + h][:, :], ACT.Identity,
                                         bias=gb1[:, 2, c:c + 1]).then_inc(mlp_act, 1)
            root(1, 4)
            for c in range(2):
                for h in range(2):
                    act.wait_ge(mlp_pe, 8 + 2 * c + h + 1)
                    nc.scalar.activation(y2[:, c, h * HALF:(h + 1) * HALF], ps[2 * c + h][:, :], ACT.Identity,
                                         bias=gb2[:, 2, c:c + 1]).then_inc(mlp_act, 1)
            root(2, 2)

        @block.vector
        def _(dve):
            v = nc.vector
            chain = [0]
            order = setup_dve_chain

            def link(i):
                chain[0] += 1
                i.then_inc(order, 1)
                dve.wait_ge(order, chain[0])

            link(v.memset(table[:, NC - 1, :, :], 0.0))
            dve.wait_ge(table_ready, 32)
            for c0, c1, kp in ((0, NC - 1, P), (NC - 1, NC, NCAT - (NC - 1) * P)):
                rest = tabf[0:kp, c0:c1, :]
                for part in range(3):
                    link(v.tensor_copy(table[0:kp, c0:c1, part, :], rest))
                    if part < 2:
                        link(v.tensor_tensor(rest, rest, table[0:kp, c0:c1, part, :], ALU.subtract))
            dve.wait_ge(consts0, 5)
            v.tensor_copy(identh[:, :], ident[:, :])
            dve.wait_ge(consts, 1)
            link(v.tensor_copy(catid[:, :], cati[:, :]))
            dve.wait_ge(weights_ready, NWD * 16)
            dve.wait_ge(consts0, 2)
            link(v.tensor_scalar(w2h[:, :, :], w2[:, :, :], 0.5, None, ALU.mult))
            link(v.tensor_copy(w2p[:, :, 0, :], w2h[:, :, :]))
            v.tensor_tensor(w2p[:, :, 1, :], w2h[:, :, :], w2p[:, :, 0, :], ALU.subtract)
            v.tensor_scalar(w3h[:, :], onesP[:, :], w3[:, 0:1], 0.5, ALU.mult, ALU.mult)
            link(v.tensor_scalar(w3r[:, :], w3[:, :], 0.5, None, ALU.mult))
            for part in range(3):
                link(v.tensor_copy(w3p[:, part:part + 1], w3r[:, :]))
                if part < 2:
                    link(v.tensor_tensor(w3r[:, :], w3r[:, :], w3p[:, part:part + 1], ALU.subtract))
            v.tensor_tensor(wac[:, :], w1[:, 0, :], w1[:, 2, :], ALU.add)
            v.tensor_tensor(wbc[:, :], w1[:, 1, :], w1[:, 2, :], ALU.subtract)
            dve.wait_ge(mask_ready, 16)
            v.tensor_scalar(valid[:, :, :], mraw, 1.0, None, ALU.is_equal)
            link(v.tensor_copy(maskf[:, :, :], mraw))
            v.tensor_scalar(off[:, :, :], valid[:, :, :], -1.0, BIG, ALU.add, ALU.mult)
            v.tensor_reduce(cnt[:, :], maskf[:, :, :], AX.X, ALU.add).then_inc(setup_dve, 1)
            dve.wait_ge(setup_pe, 1)
            for h in range(2):
                xv = xT[:, 1, :].rearrange("p (b k) -> p k b", k=BT)[:, 4 * h:4 * h + 4, :]
                uv = xT[0:E, 0, :].rearrange("p (b k) -> p k b", k=BT)[:, 4 * h:4 * h + 4, :]
                v.tensor_copy(xv, ps[h][:, :].rearrange("p (k b) -> p k b", k=4))
                i = v.tensor_copy(uv, ps[2 + h][0:E, :].rearrange("p (k b) -> p k b", k=4))
            i.then_inc(setup_dve, 1)
            dve.wait_ge(setup_pe, 2)
            link(v.tensor_copy(rcnt[:, :], ps[5][:, 64:64 + G]))
            link(v.reciprocal(rcnt[:, :], rcnt[:, :]))
            v.tensor_tensor(wmean[:, :, :], maskf[:, :, :], rcnt[:, :].unsqueeze(2).broadcast_to([P, G, J]), ALU.mult)
            v.tensor_scalar(b2f, ps[4][:, 0:1], b2v, 0.5, ALU.add, ALU.mult)
            v.tensor_scalar(b3f, ps[5][:, 0:1], b3v, None, ALU.add)
            v.tensor_scalar(vec[:, 6:8], b1v, 0.5, None, ALU.mult).then_inc(order, 1)
            chain[0] += 1
            dve.wait_ge(order, chain[0])
            dve.wait_ge(setup_pe, 3)
            for c in range(C1):
                for h in range(2):
                    i = v.tensor_scalar(cbT[:, c, h * HALF:(h + 1) * HALF], ps[2 * c + h][:, :], 0.5, vec[:, 6 + c:7 + c],
                                        ALU.mult, ALU.add)
            i.then_inc(setup_dve, 1)
            dve.wait_ge(setup_dve, 3)

            two = [(nj + 1) // 2 for _, nj in QUADS]
            CAT_TAIL = {i: sum((two * 2)[len(two) + i - 1:len(two)]) for i in range(2)}

            def effective(n, cs, q):
                if not (type(n) is int and n < WR):
                    dve.wait_ge(l1_done, n * 2 - 2 * (WR - 1))
                for r in range(2):
                    i = v.scalar_tensor_tensor(weff[:, q % WR, r, :], w1[:, 3, :], cur_s[:, cs % RING, 2 * q + r:2 * q + r + 1],
                                               wbc[:, :], ALU.mult, ALU.add)
                i.then_inc(weff_ready, 1)

            def split(n, hs, q):
                dve.wait_ge(h2_ready, n + 1)
                v.tensor_tensor(columns(h2T[:, hs % 2, 1, :], q), h2f[:, q % 2, :].rearrange("p (b j u) -> p b j u", b=2, u=U),
                                columns(h2T[:, hs % 2, 0, :], q), ALU.subtract).then_inc(h2_split, 1)

            def split1(n, q):
                for c in range(C1):
                    dve.wait_ge(h1_ready, n * 2 + (c + 1))
                    v.tensor_tensor(h1T[:, q % 2, c, 1, :], h1f[:, c, :], h1T[:, q % 2, c, 0, :],
                                    ALU.subtract).then_inc(h1_split, 1)

            def step(it, s, tr, main, back):
                g = it * RING + s
                for q in range(PAIRS):
                    if tr and q == 0:
                        dve.wait_ge(idx_ready[s], it * 32 + 32)
                        if not (type(g) is int and g < 1):
                            dve.wait_ge(row_done, g * len(QUADS))
                        v.tensor_copy(catf[:, :], idx[:, s, 1, 0:K]).then_inc(catf_ready, 1)
                    if tr and q == 0:
                        if not type(it) is int:
                            dve.wait_ge(h1_ready, (g - RING + 1) * (2 * PAIRS))
                        v.tensor_scalar(cur_s[:, s, :], xT[:, 1, bass.ds(g * GB, GB)], 1.0, None, ALU.mult)
                        v.tensor_scalar(cb_s[:, s, :, :], cbT[:, :, bass.ds(g * GB, GB)], 1.0, None,
                                        ALU.mult).then_inc(cur_out, 1)
                        if type(it) is int and s == 0:
                            dve.wait_ge(cur_out, 1)
                            effective(0, 0, 0)
                            effective(1, 0, 1)
                    if main and q < PAIRS - 2:
                        effective((g - 1) * PAIRS + q + 2, s - 1, q + 2)
                    if main and q >= PAIRS - 2 and tr:
                        if q == PAIRS - 2:
                            dve.wait_ge(cur_out, g + 1)
                        effective(g * PAIRS + q - (PAIRS - 2), s, q - (PAIRS - 2))
                    if back and q == 0 and not (type(g) is int and g < 3):
                        sums_copy(g - 3)
                    if back and q == 4:
                        dve.wait_ge(mxt_done, g - 1)
                        v.tensor_reduce(gm[:, :], mx_ps.rearrange("p (b u) -> p b u", u=U), AX.X, ALU.max).then_inc(gm_ready, 1)
                        dve.wait_ge(gm_ready, g - 1)
                        v.tensor_copy(gmx[:, :].rearrange("p (b u) -> p b u", u=U),
                                      gm[:, :].unsqueeze(2).broadcast_to([1, GB, U])).then_inc(gmx_ready, 1)
                    if tr and q in QUAD_AT:
                        i = QUAD_AT[q]
                        n = g * len(QUADS) + i
                        slot, nj = (s * len(QUADS) + i) % 2, QUADS[i][1]
                        dve.wait_ge(row_out, n + 1)
                        if not (type(n) is int and n < 2):
                            dve.wait_ge(cat_done, g * NCAT2 + (2 * (i - 2) + 2 if i >= 2 else -CAT_TAIL[i]))
                        for c in range(NC):
                            h = v.tensor_scalar(onehot[:, slot, c, 0:nj * P], catrow[:, 0:nj * P], catid[:, c:c + 1], None,
                                                ALU.is_equal)
                        h.then_inc(onehot_ready, 1)
                    if tr and q == PAIRS - 1:
                        for chunk in TR_AT[q]:
                            copy_chunk(g, s, chunk)
                    if main:
                        split1((g - 1) * PAIRS + q, q)
                    if back and q == 5:
                        dve.wait_ge(exp_done, g - 1)
                        v.tensor_scalar(rsb[:, :], blk[:, :], rs[:, 0:1], None, ALU.mult).then_inc(rsb_ready, 1)
                        v.tensor_tensor(pr[:, :], ex[:, :], maskf[:, bass.ds(g - 2, 1), :].rearrange("p a j -> p (a j)"),
                                        ALU.mult).then_inc(pr_ready, 1)
                        dve.wait_ge(pr_ready, g - 1)
                        v.tensor_tensor(wsum[:, :, 0, :], pr[:, :].unsqueeze(2).broadcast_to([P, J, GB]),
                                        blk[:, :].unsqueeze(1).broadcast_to([P, J, GB]), ALU.mult).then_inc(wsum_ready, 1)
                    if tr and q in CAT_AT:
                        i, j0, nj = CAT_AT[q]
                        dve.wait_ge(cat_done, g * NCAT2 + (j0 // 2 + 1))
                        if q == 1 and not type(it) is int:
                            dve.wait_ge(hist_free, g + 1)
                        v.tensor_reduce(hist[s][:, j0:j0 + nj, E:F],
                                        cat_ps[:, 0:nj * 3 * E].rearrange("p (j s e) -> p j e s", j=nj, s=3), AX.X,
                                        ALU.add).then_inc(cat_out, 1)
                    if back and q == 4:
                        dve.wait_ge(nmx_done, g - 1)
                        v.tensor_copy(nmx[:, :], nmx_ps).then_inc(nmx_ready, 1)
                    if tr and q in TR_AT and q < PAIRS - 1:
                        for chunk in TR_AT[q]:
                            copy_chunk(g, s, chunk)
                    if tr and q == PAIRS - 1:
                        copy_chunk(g, s, TR_LAST)
                    if q < 2 and back:
                        split((g - 1) * PAIRS - 2 + q, s, PAIRS - 2 + q)
                    if q >= 2 and main:
                        split((g - 1) * PAIRS + q - 2, s + 1, q - 2)
                    if back and q == 3:
                        v.tensor_tensor(wsum[:, :, 1, :],
                                        wmean[:, bass.ds(g - 2, 1), :].rearrange("p a j -> p (a j)").unsqueeze(2).broadcast_to([P, J, GB]),
                                        blk[:, :].unsqueeze(1).broadcast_to([P, J, GB]), ALU.mult)
                    if back and q == 2:
                        m = g - 2
                        dve.wait_ge(l3_done, g - 1)
                        v.tensor_reduce(s3[:, :], s_ps.rearrange("p (j w) -> p j w", w=3), AX.X, ALU.add).then_inc(parts_added, 1)
                        dve.wait_ge(parts_added, g - 1)
                        v.scalar_tensor_tensor(sc[:, :], s3[:, :], b3f, valid[:, bass.ds(m, 1), :].rearrange("p a j -> p (a j)"),
                                               ALU.add, ALU.mult).then_inc(biased, 1)
                        dve.wait_ge(biased, g - 1)
                        v.tensor_tensor(scm[:, :], sc[:, :], off[:, bass.ds(m, 1), :].rearrange("p a j -> p (a j)"),
                                        ALU.add).then_inc(masked, 1)
                        dve.wait_ge(masked, g - 1)
                        v.tensor_reduce(mx[:, :], scm[:, :], AX.X, ALU.max).then_inc(mx_ready, 1)

            def sums_copy(m):
                dve.wait_ge(hist_free, RING + m + 1)
                v.reciprocal(rden[:, :], den_ps).then_inc(rden_ready, 1)
                v.tensor_scalar(xT[:, 3, bass.ds(m * GB, GB)], sum_ps[:, GB:2 * GB], 1.0, None, ALU.mult)
                dve.wait_ge(rden_ready, m + 1)
                v.tensor_tensor(xT[:, 2, bass.ds(m * GB, GB)], sum_ps[:, 0:GB], rden[:, :], ALU.mult).then_inc(sums_out, 1)

            def copy_chunk(g, s, chunk):
                k = TR_ORDER.index(chunk)
                dve.wait_ge(tr_done, g * NCH + (k + 1))
                if k == 0 and not (type(g) is int and g < 2):
                    dve.wait_ge(l1_done, (g - 1) * (2 * PAIRS))
                j0, nj = chunk
                dst = histT[:, s % 2, :, :].rearrange("p b (j u) -> p j b u", u=U)[:, j0:j0 + nj, :, :]
                src = tr_ps[(s * NCH + k) % 2][:, 0:nj * P].rearrange("p (j b u) -> p j b u", j=nj, u=U)
                v.tensor_copy(dst, src).then_inc(tr_out, 1)

            for s in range(RING):
                step(0, s, True, s >= 1, s >= 2)
            with dve.Fori(1, G // RING) as it:
                for s in range(RING):
                    step(it, s, True, True, True)
            step(G // RING, 0, False, True, True)
            step(G // RING, 1, False, False, True)
            sums_copy(G - 1)
            dve.wait_ge(sums_out, G)

            def norm_scale(which, x, parts, gb):
                n = len(parts)
                link(v.memset(mv[:, :, :], 1.0))
                for c, kp in enumerate(parts):
                    for h in range(2):
                        i = v.bn_stats(st[0:kp, c, h, :], x[0:kp, c, h * HALF:(h + 1) * HALF])
                link(i)
                for c, kp in enumerate(parts):
                    i = v.bn_aggr(mv[0:kp, c, :], st[0:kp, c, :, :].rearrange("p h s -> p (h s)"))
                link(i)
                v.tensor_scalar(bs[:, 4, 0:n], mv[:, 0:n, 1], EPS, None, ALU.add).then_inc(var_ready, 1)
                dve.wait_ge(root_ready, which + 1)
                link(v.reciprocal(bs[:, 0, 0:n], bs[:, 5, 0:n]))
                link(v.tensor_tensor(bs[:, 6, 0:n], bs[:, 0, 0:n], bs[:, 0, 0:n], ALU.mult))
                link(v.tensor_tensor(bs[:, 6, 0:n], bs[:, 6, 0:n], bs[:, 4, 0:n], ALU.mult))
                link(v.tensor_scalar(bs[:, 6, 0:n], bs[:, 6, 0:n], -0.5, 1.5, ALU.mult, ALU.add))
                link(v.tensor_tensor(bs[:, 0, 0:n], bs[:, 0, 0:n], bs[:, 6, 0:n], ALU.mult))
                link(v.tensor_tensor(bs[:, 1, 0:n], bs[:, 0, 0:n], gb[:, 0, 0:n], ALU.mult))
                link(v.tensor_tensor(bs[:, 2, 0:n], mv[:, 0:n, 0], bs[:, 1, 0:n], ALU.mult))
                link(v.tensor_tensor(bs[:, 3, 0:n], gb[:, 1, 0:n], bs[:, 2, 0:n], ALU.subtract))

            dve.wait_ge(mlp_ready, NMD * 16)
            link(v.memset(gb0[E:P, :, 0:1], 1.0))
            norm_scale(0, xT, [E, P, P, P], gb0)
            for c, kp in enumerate([E, P, P, P]):
                i = v.tensor_scalar(xT[0:kp, c, :], xT[0:kp, c, :], bs[0:kp, 1, c:c + 1], bs[0:kp, 3, c:c + 1],
                                    ALU.mult, ALU.add)
            i.then_inc(bn_dve, 1)
            for which, (y, n, got, gb) in enumerate(((y1, 4, 8, gb1), (y2, 2, 12, gb2)), 1):
                dve.wait_ge(mlp_act, got)
                norm_scale(which, y, [P] * n, gb)
                for c in range(n):
                    i = v.tensor_scalar(y[:, c, :], y[:, c, :], bs[:, 1, c:c + 1], bs[:, 3, c:c + 1], ALU.mult, ALU.add)
                link(i)
                for c in range(n):
                    i = v.scalar_tensor_tensor(y[:, c, :], y[:, c, :], 0.1, y[:, c, :], ALU.mult, ALU.max)
                i.then_inc(bn_dve, 1)
            dve.wait_ge(mlp_pe, 13)
            v.tensor_tensor(outs[:, :, :], ps[4][:, 0:BT * NO].rearrange("p (k n) -> p k n", n=NO),
                            b3m[:, :].unsqueeze(1).broadcast_to([P, BT, NO]), ALU.add).then_inc(out_ready, 1)


_INS=["r_uid","r_mid","r_cat","r_historical_mid","r_historical_cat","r_mask"]+["L0_rec_"+x for x in "user_table mat_table cat_table lau_w1 lau_b1 lau_w2 lau_b2 lau_w3 lau_b3 bn0_g bn0_b mlp_w1 mlp_b1 bn1_g bn1_b mlp_w2 mlp_b2 bn2_g bn2_b mlp_w3 mlp_b3".split()]
def kernel(**inputs):
    import numpy as _np
    import concourse.bacc as _bacc
    from concourse import mybir as _mybir
    from concourse.bass_utils import run_bass_kernel_spmd as _run
    nc = _bacc.Bacc("TRN2", target_bir_lowering=False, num_devices=1)
    arrays, aps = {}, {}
    for name in _INS:
        a = _np.ascontiguousarray(inputs[name])
        arrays[f"in_{name}_dram"] = a
        aps[name]=nc.dram_tensor(f"in_{name}_dram", a.shape, _mybir.dt.from_np(a.dtype), kind="ExternalInput").ap()
    out = nc.dram_tensor("out_0_dram", (1024,2), _mybir.dt.float32, kind="ExternalOutput").ap()
    build(nc, aps, out)
    r = _run(nc, [arrays], core_ids=[0])
    return r.results[0]["out_0_dram"]
```
